# Optimizing a Trainium2 kernel written in Bass

```python
import numpy as np
import jax
import jax.numpy as jnp

def _softmax(x, axis=-1):
    return jax.nn.softmax(x, axis=axis)

def _gelu(x):
    return jax.nn.gelu(x, approximate=True)

def _silu(x):
    return jax.nn.silu(x)

def _sigmoid(x):
    return jax.nn.sigmoid(x)

def _layernorm(x, axis=-1, eps=1e-05):
    m = jnp.mean(x, axis=axis, keepdims=True)
    v = jnp.var(x, axis=axis, keepdims=True)
    return (x - m) / jnp.sqrt(v + eps)

def _scatter_add(tgt, idx, src, axis=0):
    return tgt.at[idx].add(src)

def _segment_sum(src, seg, n):
    return jax.ops.segment_sum(src, seg, n)
kernel_name = 'mk_gnn_resnorm_d2_gnn_r16_7bb477'

def setup_inputs(seed: int=0):
    np.random.seed(seed)
    _w = jnp.asarray

    def _rec_inputs():
        import jax
        import jax.numpy as jnp
        _gk = jax.random.key(seed)
        x = -8.776e-05 + 1 * jax.random.normal(jax.random.fold_in(_gk, 1), (625, 512), jnp.float32)
        src = jax.random.randint(jax.random.fold_in(_gk, 2), (10000,), 0, 625, jnp.int32)
        dst = jax.random.randint(jax.random.fold_in(_gk, 3), (10000,), 0, 625, jnp.int32)
        _o = jnp.argsort(dst, stable=True)
        src = src[_o]
        dst = dst[_o]
        edge_attr_128 = 0.000283511 + 1.00007 * jax.random.normal(jax.random.fold_in(_gk, 11), (10000, 128), jnp.float32)
        edge_type_2 = jax.random.randint(jax.random.fold_in(_gk, 13), (10000,), 0, 2, jnp.int32)
        return (x, src, dst, edge_attr_128, edge_type_2)
    x, src, dst, edge_attr_128, edge_type_2 = _rec_inputs()

    def _L0_gnn_setup():
        import jax, jax.numpy as jnp
        import numpy as np
        N, E = (625, 9375)
        HD, ED = (512, 128)
        BN_EPS = 1e-05
        key = jax.random.key(seed)
        ks = jax.random.split(key, 16)
        s = 0.02
        return {'h': jax.random.normal(ks[0], (N, HD), jnp.float32), 'edge_index': jax.random.randint(ks[1], (2, E), 0, N, jnp.int32), 'edge_attr': jax.random.normal(ks[2], (E, ED), jnp.float32), 'W1': jax.random.normal(ks[3], (HD, HD + ED), jnp.float32) * s, 'b1': jnp.zeros((HD,), jnp.float32), 'W2': jax.random.normal(ks[4], (HD, HD), jnp.float32) * s, 'b2': jnp.zeros((HD,), jnp.float32), 'W_ih': jax.random.normal(ks[5], (3 * HD, HD), jnp.float32) * s, 'W_hh': jax.random.normal(ks[6], (3 * HD, HD), jnp.float32) * s, 'b_ih': jnp.zeros((3 * HD,), jnp.float32), 'b_hh': jnp.zeros((3 * HD,), jnp.float32), 'gamma': jnp.ones((HD,), jnp.float32), 'beta': jnp.zeros((HD,), jnp.float32), 'run_mean': jnp.zeros((HD,), jnp.float32), 'run_var': jnp.ones((HD,), jnp.float32)}
    _L0_gnn_all = _L0_gnn_setup()
    _L0_gnn_in = {k: v for k, v in _L0_gnn_all.items() if k in ('W1', 'b1', 'W2', 'b2', 'W_ih', 'W_hh', 'b_ih', 'b_hh', 'gamma', 'beta', 'run_mean', 'run_var')}
    del _L0_gnn_all

    def _L1_gnn_setup():
        import jax, jax.numpy as jnp
        import numpy as np
        NUM_RELATIONS = 2
        NUM_BASES = 30
        HIDDEN = 512
        N_NODES = 625
        N_EDGES = 10000

        def rgcn_gate_layer(x, row, col, edge_type, basis, att, gate_w, root, bias):
            H = x.shape[1]
            w = jnp.einsum('rb,bio->rio', att, basis)
            x_j = x[col]
            msgs = []
            for r in range(NUM_RELATIONS):
                gate = jax.nn.sigmoid(x_j @ gate_w[r, :, 0])
                msgs.append(gate[:, None] * x_j @ w[r])
            msg = jnp.where((edge_type == 0)[:, None], msgs[0], msgs[1])
            agg = jax.ops.segment_sum(msg, row, num_segments=x.shape[0])
            return agg + x @ root + bias
        key = jax.random.key(seed)
        ks = jax.random.split(key, 16)
        H, R, B = (HIDDEN, NUM_RELATIONS, NUM_BASES)
        bound = 1.0 / np.sqrt(B * H)
        u = lambda k, shape: jax.random.uniform(k, shape, jnp.float32, -bound, bound)
        inp = {'x': jax.random.normal(ks[0], (N_NODES, H), jnp.float32), 'edge_index': jax.random.randint(ks[1], (2, N_EDGES), 0, N_NODES, jnp.int32), 'edge_type': jax.random.randint(ks[2], (N_EDGES,), 0, R, jnp.int32), 'basis1': u(ks[3], (B, H, H)), 'att1': u(ks[4], (R, B)), 'gate_w1': u(ks[5], (R, H, 1)), 'root1': u(ks[6], (H, H)), 'bias1': u(ks[7], (H,)), 'basis2': u(ks[8], (B, H, H)), 'att2': u(ks[9], (R, B)), 'gate_w2': u(ks[10], (R, H, 1)), 'root2': u(ks[11], (H, H)), 'bias2': u(ks[12], (H,))}
        return inp
    _L1_gnn_all = _L1_gnn_setup()
    _L1_gnn_in = {k: v for k, v in _L1_gnn_all.items() if k in ('basis1', 'att1', 'gate_w1', 'root1', 'bias1', 'basis2', 'att2', 'gate_w2', 'root2', 'bias2')}
    del _L1_gnn_all
    return {'x': x, 'src': src, 'dst': dst, 'edge_attr_128': edge_attr_128, 'edge_type_2': edge_type_2, 'L0_gnn_W1': _L0_gnn_in['W1'], 'L0_gnn_b1': _L0_gnn_in['b1'], 'L0_gnn_W2': _L0_gnn_in['W2'], 'L0_gnn_b2': _L0_gnn_in['b2'], 'L0_gnn_W_ih': _L0_gnn_in['W_ih'], 'L0_gnn_W_hh': _L0_gnn_in['W_hh'], 'L0_gnn_b_ih': _L0_gnn_in['b_ih'], 'L0_gnn_b_hh': _L0_gnn_in['b_hh'], 'L0_gnn_gamma': _L0_gnn_in['gamma'], 'L0_gnn_beta': _L0_gnn_in['beta'], 'L0_gnn_run_mean': _L0_gnn_in['run_mean'], 'L0_gnn_run_var': _L0_gnn_in['run_var'], 'L1_gnn_basis1': _L1_gnn_in['basis1'], 'L1_gnn_att1': _L1_gnn_in['att1'], 'L1_gnn_gate_w1': _L1_gnn_in['gate_w1'], 'L1_gnn_root1': _L1_gnn_in['root1'], 'L1_gnn_bias1': _L1_gnn_in['bias1'], 'L1_gnn_basis2': _L1_gnn_in['basis2'], 'L1_gnn_att2': _L1_gnn_in['att2'], 'L1_gnn_gate_w2': _L1_gnn_in['gate_w2'], 'L1_gnn_root2': _L1_gnn_in['root2'], 'L1_gnn_bias2': _L1_gnn_in['bias2']}

def reference(x, src, dst, edge_attr_128, edge_type_2, L0_gnn_W1, L0_gnn_b1, L0_gnn_W2, L0_gnn_b2, L0_gnn_W_ih, L0_gnn_W_hh, L0_gnn_b_ih, L0_gnn_b_hh, L0_gnn_gamma, L0_gnn_beta, L0_gnn_run_mean, L0_gnn_run_var, L1_gnn_basis1, L1_gnn_att1, L1_gnn_gate_w1, L1_gnn_root1, L1_gnn_bias1, L1_gnn_basis2, L1_gnn_att2, L1_gnn_gate_w2, L1_gnn_root2, L1_gnn_bias2):
    import jax
    import jax.numpy as jnp

    def _L0_gnn_ref(h, edge_index, edge_attr, W1, b1, W2, b2, W_ih, W_hh, b_ih, b_hh, gamma, beta, run_mean, run_var):
        import jax, jax.numpy as jnp
        import numpy as np
        N, E = (625, 9375)
        HD, ED = (512, 128)
        BN_EPS = 1e-05
        src, dst = (edge_index[0], edge_index[1])
        m_in = jnp.concatenate([h[src], edge_attr], axis=1)
        m = jax.nn.relu(m_in @ W1.T + b1) @ W2.T + b2
        agg = jax.ops.segment_sum(m, dst, num_segments=h.shape[0])
        gi = agg @ W_ih.T + b_ih
        gh = h @ W_hh.T + b_hh
        i_r, i_z, i_n = jnp.split(gi, 3, axis=1)
        h_r, h_z, h_n = jnp.split(gh, 3, axis=1)
        r = jax.nn.sigmoid(i_r + h_r)
        z = jax.nn.sigmoid(i_z + h_z)
        n = jnp.tanh(i_n + r * h_n)
        h_new = (1.0 - z) * n + z * h
        bn = gamma * (h_new - run_mean) * jax.lax.rsqrt(run_var + BN_EPS) + beta
        return h + bn

    def _L1_gnn_ref(x, edge_index, edge_type, basis1, att1, gate_w1, root1, bias1, basis2, att2, gate_w2, root2, bias2):
        import jax, jax.numpy as jnp
        import numpy as np
        NUM_RELATIONS = 2
        NUM_BASES = 30
        HIDDEN = 512
        N_NODES = 625
        N_EDGES = 10000

        def rgcn_gate_layer(x, row, col, edge_type, basis, att, gate_w, root, bias):
            H = x.shape[1]
            w = jnp.einsum('rb,bio->rio', att, basis)
            x_j = x[col]
            msgs = []
            for r in range(NUM_RELATIONS):
                gate = jax.nn.sigmoid(x_j @ gate_w[r, :, 0])
                msgs.append(gate[:, None] * x_j @ w[r])
            msg = jnp.where((edge_type == 0)[:, None], msgs[0], msgs[1])
            agg = jax.ops.segment_sum(msg, row, num_segments=x.shape[0])
            return agg + x @ root + bias
        row, col = (edge_index[0], edge_index[1])
        h = jax.nn.relu(rgcn_gate_layer(x, row, col, edge_type, basis1, att1, gate_w1, root1, bias1))
        out = rgcn_gate_layer(h, row, col, edge_type, basis2, att2, gate_w2, root2, bias2)
        return out
    edge_index = jnp.stack([src, dst])
    x = _layernorm(x + _L0_gnn_ref(x, edge_index, edge_attr_128, L0_gnn_W1, L0_gnn_b1, L0_gnn_W2, L0_gnn_b2, L0_gnn_W_ih, L0_gnn_W_hh, L0_gnn_b_ih, L0_gnn_b_hh, L0_gnn_gamma, L0_gnn_beta, L0_gnn_run_mean, L0_gnn_run_var), axis=-1)
    x = _layernorm(x + _L1_gnn_ref(x, edge_index, edge_type_2, L1_gnn_basis1, L1_gnn_att1, L1_gnn_gate_w1, L1_gnn_root1, L1_gnn_bias1, L1_gnn_basis2, L1_gnn_att2, L1_gnn_gate_w2, L1_gnn_root2, L1_gnn_bias2), axis=-1)
    return x

_drawn_inputs = setup_inputs


def setup_inputs(seed=0):
    import zlib

    import numpy as np

    out = dict(_drawn_inputs(seed))
    spreads = {'L0_gnn_b1': (0.0, 0.1),
     'L0_gnn_b2': (0.0, 0.1),
     'L0_gnn_b_ih': (0.0, 0.436),
     'L0_gnn_b_hh': (0.0, 0.635),
     'L0_gnn_gamma': (1.0, 0.2),
     'L0_gnn_beta': (0.0, 0.1),
     'L0_gnn_run_mean': (0.0, 0.1),
     'L0_gnn_run_var': (1.0, 0.6)}
    factors = {'L1_gnn_basis1': 8.0,
     'L1_gnn_att1': 8.0,
     'L1_gnn_gate_w1': 8.0,
     'L1_gnn_root1': 8.0,
     'L1_gnn_bias1': 8.0,
     'L1_gnn_basis2': 8.0,
     'L1_gnn_att2': 8.0,
     'L1_gnn_gate_w2': 8.0,
     'L1_gnn_root2': 7.264,
     'L1_gnn_bias2': 8.0}
    for name, (base, spread) in spreads.items():
        noise = np.random.default_rng([zlib.crc32(name.encode()), seed]).standard_normal(out[name].shape)
        drawn = base * np.exp(spread * noise) if base else spread * noise
        out[name] = jnp.asarray(drawn.astype(out[name].dtype))
    for name, factor in factors.items():
        out[name] = (out[name] * factor).astype(out[name].dtype)
    return out
```

```python
from contextlib import ExitStack

import numpy as np

import concourse.bass as bass
from concourse import mybir
from concourse.alu_op_type import AluOpType as ALU

ACT = mybir.ActivationFunctionType
AX = mybir.AxisListType
F32 = mybir.dt.float32
F32R = mybir.dt.float32r
F16 = mybir.dt.float16
BF16 = mybir.dt.bfloat16
I32 = mybir.dt.int32

P = 128
N = 625
NT = 5
NP = NT * P
E = 10000
ET = 80
H = 512
KT = H // P
ED = 128
BASES = 30
REL = 2
UNROLL = 8
EA_TILES = 4
QTR = 4
BK = BASES * QTR
CONSTS = 13
WT = H // (QTR * 16)
HALF = NP // 2
RN = REL * NP
BN_EPS = 1e-5
LN_EPS = 1e-5
SLOTS = 2


def plan_jobs():
    jobs = [(("RT", n), "AV"[n % 2]) for n in range(NT)]
    jobs += [(("cnt", 0), "V"), (("cnt", 1), "V")]
    jobs += [(("agg", o, h), "AV"[h]) for o in range(KT) for h in range(2)]
    w = 0
    for n in range(NT):
        jobs += [(("r", n), "A"), (("z", n), "A")]
        if w < WT:
            jobs.append((("w", 0, w), "A"))
            w += 1
        jobs += [(("hn", n), "V"), (("in", n), "V")]
        if w < WT:
            jobs.append((("w", 0, w), "A"))
            w += 1
    for layer in range(2):
        jobs += [(("xT", layer, n), "A") for n in range(NT)]
        jobs += [(("gate", layer), "A")]
        if layer == 0:
            jobs += [(("w", 1, t), "A") for t in range(2)]
        for q in range(2 * REL * KT):
            jobs.append((("Z", layer, q // 8, q // 2 % 4, q % 2), "AV"[q % 2]))
            if layer == 0 and q % 4 == 3:
                jobs.append((("w", 1, 2 + q // 4), "A"))
        for n in range(NT):
            jobs.append((("out", layer, n), "AV"[layer]))
        if layer == 0:
            jobs += [(("w", 1, t), "A") for t in (6, 7)]
    return jobs


class Jobs:

    def __init__(self):
        self.list = plan_jobs()
        self.at = {name: n for n, (name, _) in enumerate(self.list)}
        self.drains = {}
        count = {"A": 0, "V": 0}
        for name, e in self.list:
            count[e] += 1
            self.drains[name] = (e, count[e])

    def bank(self, name):
        return self.at[name] % 8


def gnn_kernel(nc, t):
    jobs = Jobs()
    ctx = ExitStack()
    with ctx:
        def sb(name, shape, dt=F32):
            return ctx.enter_context(nc.sbuf_tensor(name, shape, dt))

        def sem(name):
            return ctx.enter_context(nc.semaphore(name))

        x_sb = sb("x_sb", [P, NT, H])
        xT = sb("xT", [P, KT, NP])
        x1 = sb("x1", [P, NT, H])
        CT = sb("CT", [P, NT, RN])
        basis = sb("basis", [BK, SLOTS, QTR, 2, H])
        R = sb("R", [P, NT * H])
        RT = sb("RT", [P, KT, NP])
        W2T = sb("W2T", [P, KT, H])
        bn = sb("bn", [P, 2, H])
        ev = sb("ev", [P, 2, H])
        X = sb("X", [P, 14 * 1024])
        rhi = sb("rhi", [P, 2, H], F32R)
        rlo = sb("rlo", [P, 2, H], F32R)
        oh = sb("oh", [P, 2, P], F32R)
        iota = sb("iota", [P, RN], F16)
        ident = sb("ident", [P, P])
        esrc = sb("esrc", [P, ET], I32)
        edst = sb("edst", [P, ET], I32)
        etyp = sb("etyp", [P, ET], I32)
        dstf = sb("dstf", [P, ET])
        keyf = sb("keyf", [P, ET])
        srcf = sb("srcf", [P, ET])
        idx = sb("idx", [P, 4], I32)
        rows = ev[0:1].rearrange("p s n -> p (s n)")
        gbias = sb("gbias", [2, 3 * H])
        rbias = sb("rbias", [1, 2, H])
        ones = sb("ones", [2, P])
        pick = sb("pick", [2, P])
        zer = RT[:, 0, 0:H // 2].bitcast(BF16)
        cnt = sb("cnt", [P, NT])
        cntrow = iota[0:1, :].bitcast(F32)
        maskc = sb("maskc", [BK, QTR])
        att = sb("att", [BK, 2, REL])
        sel = sb("sel", [BK, 2, 4, 32])
        gw = sb("gw", [P, 2, KT, REL])
        gate = sb("gate", [P, 2, 2 * NT])
        stat = sb("stat", [P, 2, 6])
        mv = sb("mv", [P, 2, 2])
        sd = sb("sd", [P, 2, 2])
        epst = sb("epst", [P, 1])

        ps = ctx.enter_context(nc.psum_tensor("ps", [P, 8, 512], F32))
        flat = ps[:].rearrange("p b n -> p (b n)")

        eaT = X[:, 0:1024].rearrange("p (s n) -> p s n", s=2)
        gat = X[:, 1024:3072].rearrange("p (s n) -> p s n", s=4)
        pre = X[:, 3072:4096].rearrange("p (s n) -> p s n", s=2)
        W1bT = X[:, 4096:4608]
        W1aT = X[:, 4608:6656].rearrange("p (k n) -> p k n", k=KT)
        u_sb = X[:, 6656:9216].rearrange("p (k n) -> p k n", k=NT)
        ohs = X[:, 9216:10496].bitcast(BF16).rearrange("p (s n) -> p s n", s=2)
        ohd = X[:, 10496:10624].bitcast(BF16).rearrange("p (s n) -> p s n", s=2)
        WihT = X[:, 0:6144].rearrange("p (k n) -> p k n", k=KT)
        WhhT = X[:, 6144:12288].rearrange("p (k n) -> p k n", k=KT)
        gru = X[:, 12288:14336].rearrange("p (s n) -> p s n", s=4)
        w_sb = X[:, 0:4096].rearrange("p (r k n) -> p r k n", r=REL, k=KT)
        y_sb = X[:, 4096:9216].rearrange("p (m r n) -> p m r n", m=NT, r=REL)
        ZT = X[:, 9216:14336].rearrange("p (q n) -> p q n", q=2 * KT)
        aggT = R[:, :].rearrange("p (k n) -> p k n", k=KT)
        R_v = R[:, :].rearrange("p (m n) -> p m n", m=NT)
        h1 = x_sb
        root = [W2T[:, :, :], xT[:, :, 0:H]]
        lnw = bn

        idx_in = sem("idx_in")
        const_in = sem("const_in")
        u_in = sem("u_in")
        x_in = sem("x_in")
        w1b_in = sem("w1b_in")
        w2_in = sem("w2_in")
        gru_in = sem("gru_in")
        ea_in = [sem(f"ea_in{i}") for i in range(2)]
        gat_in = [sem(f"gat_in{i}") for i in range(4)]
        basis_in = [sem(f"basis_in{i}") for i in range(SLOTS)]
        root_in = [sem("root_in0"), sem("root_in1")]
        w_in = sem("w_in")
        w_out = [sem("w_out0"), sem("w_out1")]
        u_out = sem("u_out")
        y_out = sem("y_out")
        dve_step = sem("dve_step")
        keys_ready = sem("keys_ready")
        setup_ready = sem("setup_ready")
        hot_ready = sem("hot_ready")
        hot_free = sem("hot_free")
        ct_acc = sem("ct_acc")
        ct_drained = sem("ct_drained")
        u_acc = sem("u_acc")
        u_drained = sem("u_drained")
        ea_done = sem("ea_done")
        pre_ready = sem("pre_ready")
        hi_ready = sem("hi_ready")
        lo_ready = sem("lo_ready")
        oh_ready = sem("oh_ready")
        oh_free = sem("oh_free")
        r_acc = sem("r_acc")
        var_ready = sem("var_ready")
        std_ready = sem("std_ready")
        r_drained = sem("r_drained")
        bank_full = sem("bank_full")
        drained = {"A": sem("act_drained"), "V": sem("dve_drained")}
        basis_used = sem("basis_used")
        n_ready = sem("n_ready")
        x1_sum = sem("x1_sum")
        sd_ready = sem("sd_ready")
        x1_ready = sem("x1_ready")
        cnt_ready = sem("cnt_ready")
        y_ready = [sem("y_ready0"), sem("y_ready1")]
        out_ready = sem("out_ready")

        def drained_by(eng, name):
            e, n = jobs.drains[name]
            eng.wait_ge(drained[e], n)

        def full(eng, name):
            eng.wait_ge(bank_full, jobs.at[name] + 1)

        block = ctx.enter_context(nc.Block())

        @block.sync
        def _(sp):
            for a, b in ((esrc, t["src"]), (edst, t["dst"]), (etyp, t["typ"])):
                sp.dma_start(a[:], b).then_inc(idx_in, 16)
            for a, b in ((iota, t["iota"]), (ident, t["ident"]), (rows, t["rows"]), (pick, t["pick"]), (gbias, t["gbias"]),
                         (rbias, t["rbias"]), (maskc, t["maskc"]), (att, t["att"]), (gw, t["gw"])):
                sp.dma_start(a[:], b).then_inc(const_in, 16)
            for i, a in enumerate(t["bn"]):
                sp.dma_start(gru[:, i], a.broadcast_to([P, H])).then_inc(const_in, 16)
            sp.dma_start(xT[:], t["xT"]).then_inc(u_in, 16)
            sp.dma_start(W1aT, t["W1aT"]).then_inc(u_in, 16)
            sp.dma_start(W1bT, t["W1bT"]).then_inc(w1b_in, 16)
            sp.dma_start(x_sb[:], t["x"]).then_inc(x_in, 16)
            sp.dma_start(W2T[:], t["W2T"]).then_inc(w2_in, 16)

            def load_basis(c):
                layer, tile, half = c // (2 * WT), c // 2 % WT, c % 2
                if c >= SLOTS:
                    old = c - SLOTS
                    if old % 2:
                        full(sp, ("w", old // (2 * WT), old // 2 % WT))
                    else:
                        sp.wait_ge(basis_used, old // 2 + 1)
                src = t["basis"][layer].rearrange(
                    "b (c w g h s) o -> (b c) w g h (s o)", c=QTR, w=WT, g=4, h=2)[:, tile, :, half]
                sp.dma_start(basis[:, c % SLOTS].rearrange("p g s o -> p g (s o)"),
                             src).then_inc(basis_in[c % SLOTS], 16)

            for c in range(SLOTS):
                load_basis(c)
            for n in range(NT):
                sp.wait_ge(u_drained, n + 1)
                sp.dma_start(t["u"][n * P:(n + 1) * P, :], u_sb[:, n]).then_inc(u_out, 16)
            with sp.Fori(0, ET // UNROLL) as it:
                for s in range(2):
                    sp.wait_ge(ea_done, it * UNROLL + EA_TILES * (s + 1))
                    sp.dma_start(eaT[:, s], t["eaT"][:, bass.ds(it * (UNROLL * P) + s * H, H)]
                                 ).then_inc(ea_in[s], 16)
            sp.wait_ge(r_drained, NT)
            sp.dma_start(WihT, t["WihT"]).then_inc(gru_in, 16)
            sp.dma_start(WhhT, t["WhhT"]).then_inc(gru_in, 16)

            nb = SLOTS
            for name, _ in jobs.list:
                if name[0] == "w":
                    _, layer, tile = name
                    for _ in range(2):
                        if nb < 2 * WT * 2:
                            load_basis(nb)
                            nb += 1
                    drained_by(sp, name)
                    sp.dma_start(t["w"][layer][tile], ev[:, tile % 2]).then_inc(w_out[tile % 2], 16)
                    if tile == WT - 1:
                        for s in range(2):
                            sp.wait_ge(w_out[s], 16 * (layer + 1) * WT // 2)
                        if layer == 0:
                            full(sp, ("in", NT - 1))
                        else:
                            full(sp, ("out", 0, NT - 1))
                        for r in range(REL):
                            for k in range(KT):
                                src = t["w"][layer][2 * k:2 * k + 2].rearrange(
                                    "w (g r c) o -> (w g) r c o", g=4, r=REL)[:, r]
                                sp.dma_start(w_sb[:, r, k], src).then_inc(w_in, 16)
                if name == ("agg", KT - 1, 1):
                    full(sp, name)
                    sp.dma_start(root[0], t["root"][0]).then_inc(root_in[0], 16)
                if name == ("gate", 0):
                    full(sp, ("in", NT - 1))
                    sp.dma_start(root[1], t["root"][1]).then_inc(root_in[1], 16)
            for n in range(NT):
                sp.wait_ge(out_ready, n + 1)
                sp.dma_start(t["out"][n * P:(n + 1) * P, :], h1[:, n]).then_inc(y_out, 16)
            sp.wait_ge(y_out, 16 * NT)
            sp.wait_ge(u_out, 16 * NT)

        @block.gpsimd
        def _(pool):
            pool.wait_ge(idx_in, 48)
            pool.wait_ge(u_out, 16 * NT)
            with pool.Fori(0, ET // UNROLL) as it:
                for s in range(UNROLL):
                    pool.wait_ge(pre_ready, it * UNROLL + s + 1)
                    nc.gpsimd.tensor_copy(idx[:, s % 4:s % 4 + 1],
                                          esrc[:, bass.ds(it * UNROLL + s, 1)])
                    pool.drain()
                    nc.gpsimd.indirect_dma_start(
                        gat[:, s % 4], None, t["u"][:, :],
                        bass.IndirectOffsetOnAxis(ap=idx[:, s % 4:s % 4 + 1], axis=0)
                        ).then_inc(gat_in[s % 4], 16)

        @block.scalar
        def _(act):
            act.wait_ge(var_ready, 1)
            nc.scalar.activation(bn[:, 0], bn[:, 1], ACT.Sqrt).then_inc(std_ready, 1)
            for j in range(NT):
                act.wait_ge(ct_acc, j + 1)
                b = 3 * (j % 2) * 512
                nc.scalar.copy(CT[:, j], flat[:, b:b + RN]).then_inc(ct_drained, 1)
            for n in range(NT):
                act.wait_ge(u_acc, n + 1)
                nc.scalar.copy(u_sb[:, n], ps[:, 5 + n % 3]).then_inc(u_drained, 1)
            with act.Fori(0, ET // UNROLL) as it:
                for s in range(UNROLL):
                    act.wait_ge(pre_ready, it * UNROLL + s + 5)
                    nc.scalar.activation(rhi[:, s % 2], pre[:, s % 2], ACT.Relu).then_inc(hi_ready, 1)
            for n in range(NT):
                act.wait_ge(r_acc, 1)
                nc.scalar.copy(R_v[:, n], ps[:, n]).then_inc(r_drained, 1)
            nw = 0
            for name, e in jobs.list:
                kind = name[0]
                bank = ps[:, jobs.bank(name)]
                if kind == "w":
                    if nw >= 2:
                        act.wait_ge(w_out[nw % 2], 16 * (nw // 2))
                if e == "A":
                    full(act, name)
                    if kind == "RT":
                        ins = nc.scalar.copy(RT[:, :, name[1] * P:(name[1] + 1) * P],
                                             bank.rearrange("p (k n) -> p k n", k=KT))
                    elif kind == "agg":
                        ins = nc.scalar.copy(aggT[:, name[1], 0:HALF], bank[:, 0:HALF])
                    elif kind in "rz":
                        if name[1] >= 1:
                            act.wait_ge(x1_sum, name[1])
                        ins = nc.scalar.activation(gru[:, "rz".index(kind)], bank, ACT.Sigmoid)
                    elif kind == "w":
                        ins = nc.scalar.copy(ev[:, nw % 2], bank)
                        nw += 1
                    elif kind == "xT":
                        ins = nc.scalar.copy(RT[:, :, name[2] * P:(name[2] + 1) * P],
                                             bank.rearrange("p (k n) -> p k n", k=KT))
                    elif kind == "gate":
                        ins = nc.scalar.activation(gate[:, name[1]], bank[:, 0:2 * NT], ACT.Sigmoid)
                    elif kind == "Z":
                        ins = nc.scalar.copy(ZT[:, name[2] * KT + name[3], 0:HALF], bank[:, 0:HALF])
                    elif kind == "out":
                        ins = nc.scalar.activation(h1[:, name[2]], bank, ACT.Relu)
                    ins.then_inc(drained["A"], 1)
                if kind == "in":
                    drained_by(act, name)
                    nc.scalar.activation(gru[:, 3], gru[:, 2], ACT.Tanh).then_inc(n_ready, 1)
                    act.wait_ge(x1_sum, name[1] + 1)
                    nc.scalar.activation(sd[:, 0, 0:1], mv[:, 0, 1:2], ACT.Sqrt,
                                         bias=epst[:, 0:1]).then_inc(sd_ready, 1)
                if kind == "out" and name[1] == 1:
                    act.wait_ge(x1_sum, NT + name[2] + 1)
                    nc.scalar.activation(sd[:, 0, 0:1], mv[:, 0, 1:2], ACT.Sqrt,
                                         bias=epst[:, 0:1]).then_inc(sd_ready, 1)

        @block.vector
        def _(dve):
            steps = [0]

            def step(ins):
                steps[0] += 1
                ins.then_inc(dve_step, 1)
                dve.wait_ge(dve_step, steps[0])

            dve.memset(zer, 0.0)
            dve.memset(ones[:], 1.0)
            dve.memset(epst[:], LN_EPS)
            step(dve.memset(sel[:], 0.0))
            dve.wait_ge(idx_in, 48)
            dve.tensor_copy(srcf[:], esrc[:])
            dve.tensor_copy(dstf[:], edst[:])
            step(dve.tensor_copy(keyf[:], etyp[:]))
            step(dve.tensor_scalar(keyf[:], keyf[:], 0.0, float(NP), ALU.not_equal, ALU.mult))
            step(dve.tensor_tensor(keyf[:], keyf[:], srcf[:], ALU.add))
            dve.wait_ge(const_in, 16 * CONSTS)
            step(dve.tensor_scalar(bn[:, 1], gru[:, 3], BN_EPS, None, ALU.add))
            dve.nop().then_inc(var_ready, 1)
            dve.wait_ge(std_ready, 1)
            step(dve.reciprocal(bn[:, 1], bn[:, 0]))
            step(dve.tensor_tensor(bn[:, 0], bn[:, 1], gru[:, 0], ALU.mult))
            step(dve.tensor_tensor(bn[:, 1], bn[:, 0], gru[:, 2], ALU.mult))
            step(dve.tensor_tensor(bn[:, 1], gru[:, 1], bn[:, 1], ALU.subtract))
            for layer in range(2):
                for r in range(REL):
                    for s in range(4):
                        last = dve.tensor_scalar(sel[:, layer, s, 16 * r + s:16 * r + 16:4], maskc[:],
                                                 att[:, layer, r:r + 1], None, ALU.mult)
            last.then_inc(setup_ready, 1)
            for j in range(NT):
                with dve.Fori(0, ET // 2) as it:
                    for s in range(2):
                        dve.wait_ge(hot_free, it * 2 + j * ET + s + 1)
                        dve.tensor_scalar(ohs[:, s], iota[:], keyf[:, bass.ds(it * 2 + s, 1)], None,
                                          ALU.is_equal)
                        dve.tensor_scalar(ohd[:, s], iota[:, j * P:(j + 1) * P],
                                          dstf[:, bass.ds(it * 2 + s, 1)], None,
                                          ALU.is_equal).then_inc(hot_ready, 1)
            dve.nop().then_inc(pre_ready, 4)
            dve.nop().then_inc(lo_ready, 2)
            with dve.Fori(0, ET // UNROLL) as it:
                for s in range(UNROLL):
                    dve.wait_ge(ea_done, it * UNROLL + UNROLL + s + 1)
                    dve.wait_ge(gat_in[s % 4], (it * 2 + s // 4 + 1) * 16)
                    dve.wait_ge(lo_ready, it * UNROLL + s + 1)
                    dve.tensor_tensor(pre[:, s % 2], ps[:, 5 + s % 2], gat[:, s % 4],
                                      ALU.add).then_inc(pre_ready, 1)
                    for j in range(NT):
                        w = (s * NT + j) % 2
                        dve.wait_ge(oh_free, it * (UNROLL * NT) + s * NT + j + 1)
                        dve.tensor_scalar(oh[:, w], iota[:, j * P:(j + 1) * P],
                                          dstf[:, bass.ds(it * UNROLL + s, 1)], None,
                                          ALU.is_equal).then_inc(oh_ready, 1)
                        if j == 0:
                            dve.wait_ge(hi_ready, it * UNROLL + s + 1)
                            nc.vector.scalar_tensor_tensor(
                                out=rlo[:, s % 2], in0=pre[:, s % 2], scalar=0.0,
                                in1=rhi[:, s % 2].bitcast(F32), op0=ALU.max,
                                op1=ALU.subtract).then_inc(lo_ready, 1)
            dve.wait_ge(ct_drained, NT)
            for n in range(NT):
                last = dve.tensor_reduce(cnt[:, n:n + 1], CT[:, n], AX.X, ALU.add)
            last.then_inc(cnt_ready, 1)
            def layer_norm(rows_in, rows_out, turn, done):
                dve_bn = dve.bn_stats(stat[:, 0], rows_in)
                step(dve_bn)
                dve.bn_aggr(mv[:, 0], stat[:, 0]).then_inc(x1_sum, 1)
                dve.wait_ge(sd_ready, turn + 1)
                step(dve.reciprocal(sd[:, 0, 1:2], sd[:, 0, 0:1]))
                dve.tensor_scalar(rows_out, rows_in, mv[:, 0, 0:1], sd[:, 0, 1:2], ALU.subtract,
                                  ALU.mult).then_inc(done, 1)

            for name, e in jobs.list:
                kind = name[0]
                bank = ps[:, jobs.bank(name)]
                if e == "V":
                    full(dve, name)
                    if kind == "RT":
                        ins = dve.tensor_copy(RT[:, :, name[1] * P:(name[1] + 1) * P],
                                              bank.rearrange("p (k n) -> p k n", k=KT))
                    elif kind == "cnt":
                        a, b = ((0, 3), (3, NT))[name[1]]
                        ins = dve.tensor_copy(cntrow[0:1, a * P:b * P], bank[0:1, 0:(b - a) * P])
                    elif kind == "agg":
                        ins = dve.tensor_copy(aggT[:, name[1], HALF:NP], bank[:, 0:HALF])
                    elif kind == "hn":
                        drained_by(dve, ("r", name[1]))
                        ins = dve.tensor_tensor(gru[:, 2], bank, gru[:, 0], ALU.mult)
                    elif kind == "in":
                        drained_by(dve, ("hn", name[1]))
                        ins = dve.tensor_tensor(gru[:, 2], bank, gru[:, 2], ALU.add)
                    elif kind == "Z":
                        ins = dve.tensor_copy(ZT[:, name[2] * KT + name[3], HALF:NP], bank[:, 0:HALF])
                    elif kind == "out":
                        ins = dve.tensor_tensor(h1[:, name[2]], bank, x1[:, name[2]], ALU.add)
                    ins.then_inc(drained["V"], 1)
                if kind == "in":
                    n = name[1]
                    drained_by(dve, name)
                    dve.wait_ge(n_ready, n + 1)
                    drained_by(dve, ("z", n))
                    dve.wait_ge(x_in, 16)
                    step(dve.tensor_tensor(gru[:, 2], x_sb[:, n], gru[:, 3], ALU.subtract))
                    step(dve.tensor_tensor(gru[:, 2], gru[:, 1], gru[:, 2], ALU.mult))
                    step(dve.tensor_tensor(gru[:, 3], gru[:, 2], gru[:, 3], ALU.add))
                    step(dve.tensor_tensor(gru[:, 2], gru[:, 3], bn[:, 0], ALU.mult))
                    step(dve.tensor_tensor(gru[:, 2], gru[:, 2], bn[:, 1], ALU.add))
                    step(nc.vector.scalar_tensor_tensor(out=gru[:, 3], in0=x_sb[:, n], scalar=2.0,
                                                        in1=gru[:, 2], op0=ALU.mult, op1=ALU.add))
                    layer_norm(gru[:, 3], x1[:, n], n, x1_ready)
                if kind == "gate":
                    layer = name[1]
                    src = (x1, h1)[layer]
                    drained_by(dve, name)
                    if layer == 0:
                        full(dve, ("in", NT - 1))
                        dve.wait_ge(x1_ready, NT)
                    else:
                        full(dve, ("Z", 0, 1, KT - 1, 1))
                    for m in range(NT):
                        for r in range(REL):
                            dve.tensor_scalar(y_sb[:, m, r].rearrange("p (u c s) -> p u c s", c=QTR, s=4),
                                              src[:, m].rearrange("p (c u s) -> p u c s", c=QTR, s=4),
                                              gate[:, layer, 2 * m + r:2 * m + r + 1],
                                              None, ALU.mult).then_inc(y_ready[layer], 1)
                if kind == "out" and name[1] == 1:
                    drained_by(dve, name)
                    layer_norm(h1[:, name[2]], h1[:, name[2]], NT + name[2], out_ready)

        @block.tensor
        def _(pe):
            pe.nop().then_inc(hot_free, 2)
            pe.wait_ge(setup_ready, 1)
            for j in range(NT):
                if j >= 2:
                    pe.wait_ge(ct_drained, j - 1)
                banks = [ps[:, 3 * (j % 2) + c, 0:min(512, RN - 512 * c)] for c in range(3)]
                for c in range(3):
                    w = banks[c].shape[1]
                    pe.matmul(banks[c], zer[:, 0:P], zer[:, 0:w], start=True, stop=True)
                with pe.Fori(0, ET // 2) as it:
                    for s in range(2):
                        pe.wait_ge(hot_ready, it * 2 + j * ET + s + 1)
                        for c in range(3):
                            w = banks[c].shape[1]
                            mm = pe.matmul(banks[c], ohd[:, s], ohs[:, s, 512 * c:512 * c + w],
                                           start=False, stop=True, skip_group_check=True)
                        mm.then_inc(hot_free, 1)
                pe.matmul(banks[2], zer[:, 0:P], zer[:, 0:w], start=False, stop=True,
                          skip_group_check=True).then_inc(ct_acc, 1)
            pe.wait_ge(u_in, 32)
            pe.wait_ge(ct_drained, 4)
            for n in range(NT):
                if n >= 3:
                    pe.wait_ge(u_drained, n - 2)
                bank = ps[:, 5 + n % 3]
                pe.matmul(bank, ones[0:1, :], rows[0:1, 0:H], start=True, stop=False)
                for k in range(KT):
                    mm = pe.matmul(bank, xT[:, k, n * P:(n + 1) * P], W1aT[:, k], start=False,
                                   stop=(k == KT - 1))
                mm.then_inc(u_acc, 1)
            pe.wait_ge(ct_drained, NT)
            pe.wait_ge(u_drained, NT)
            pe.wait_ge(w1b_in, 16)
            for n in range(NT):
                pe.matmul(ps[:, n], zer[:, 0:P], zer, start=True, stop=True)
            pe.nop().then_inc(ea_done, UNROLL)
            pe.nop().then_inc(oh_free, 2)

            def attributes(it, s):
                if s % EA_TILES == 0:
                    pe.wait_ge(ea_in[s // EA_TILES % 2], (it + s // UNROLL + 1) * 16)
                pe.wait_ge(pre_ready, it * UNROLL + s + 3)
                col = s % UNROLL % EA_TILES * P
                pe.matmul(ps[:, 5 + s % 2], eaT[:, s // EA_TILES % 2, col:col + P], W1bT,
                          start=True, stop=True).then_inc(ea_done, 1)

            def turn(it, ahead):
                for s in range(UNROLL):
                    pe.wait_ge(lo_ready, it * UNROLL + s + 3)
                    for j in range(NT):
                        w = (s * NT + j) % 2
                        pe.wait_ge(oh_ready, it * (UNROLL * NT) + s * NT + j + 1)
                        pe.matmul(ps[:, j], oh[:, w], rhi[:, s % 2], start=False, stop=True,
                                  skip_group_check=True)
                        pe.matmul(ps[:, j], oh[:, w], rlo[:, s % 2], start=False, stop=True,
                                  skip_group_check=True).then_inc(oh_free, 1)
                    if s < ahead:
                        attributes(it, s + 2)

            attributes(0, 0)
            attributes(0, 1)
            with pe.Fori(0, ET // UNROLL - 1) as it:
                turn(it, UNROLL)
            turn(ET // UNROLL - 1, UNROLL - 2)
            pe.matmul(ps[:, 7, 0:64], zer[:, 0:P], zer[:, 0:64], start=True, stop=True).then_inc(r_acc, 1)

            nb = 0
            for n, (name, _) in enumerate(jobs.list):
                kind = name[0]
                bank = ps[:, jobs.bank(name)]
                if n >= 8:
                    drained_by(pe, jobs.list[n - 8][0])
                if kind == "RT":
                    pe.wait_ge(r_drained, NT)
                    for k in range(KT):
                        mm = pe.transpose(bank[:, k * P:(k + 1) * P], R_v[:, name[1], k * P:(k + 1) * P],
                                          ident[:])
                elif kind == "cnt":
                    pe.wait_ge(cnt_ready, 1)
                    a, b = ((0, 3), (3, NT))[name[1]]
                    for m in range(a, b):
                        mm = pe.matmul(bank[0:1, (m - a) * P:(m - a + 1) * P], cnt[:, m:m + 1], ident[:],
                                       start=True, stop=True)
                elif kind == "agg":
                    _, o, h = name
                    if (o, h) == (0, 0):
                        for q in range(NT):
                            drained_by(pe, ("RT", q))
                        drained_by(pe, ("cnt", 1))
                        pe.wait_ge(w2_in, 16)
                    cols = slice(h * HALF, (h + 1) * HALF)
                    pe.matmul(bank[:, 0:HALF], rows[0:1, H + o * P:H + (o + 1) * P], cntrow[0:1, cols],
                              start=True, stop=False)
                    for k in range(KT):
                        mm = pe.matmul(bank[:, 0:HALF], W2T[:, k, o * P:(o + 1) * P], RT[:, k, cols],
                                       start=False, stop=(k == KT - 1))
                elif kind in ("r", "z", "hn", "in"):
                    m = name[1]
                    if kind == "r" and m == 0:
                        pe.wait_ge(gru_in, 32)
                        drained_by(pe, ("agg", KT - 1, 0))
                        drained_by(pe, ("agg", KT - 1, 1))
                    q = {"r": 0, "z": 1, "hn": 2, "in": 2}[kind]
                    cols = slice(q * H, (q + 1) * H)
                    K = 2 if kind in "rz" else 1
                    if kind == "hn":
                        pe.matmul(bank, pick[:], gbias[:, cols], start=True, stop=False)
                    else:
                        pe.matmul(bank, ones[0:K, :], gbias[0:K, cols], start=True, stop=False)
                    parts = [(aggT, WihT)] * (kind != "hn") + [(xT, WhhT)] * (kind != "in")
                    for i, (a, w) in enumerate(parts):
                        for k in range(KT):
                            mm = pe.matmul(bank, a[:, k, m * P:(m + 1) * P], w[:, k, cols], start=False,
                                           stop=(i == len(parts) - 1 and k == KT - 1))
                elif kind == "w":
                    _, layer, tile = name
                    for half in range(2):
                        pe.wait_ge(basis_in[nb % SLOTS], 16 * (nb // SLOTS + 1))
                        for s2 in range(2):
                            s = 2 * half + s2
                            for g in range(4):
                                mm = pe.matmul(bank[32 * g:32 * g + 32], sel[:, layer, s],
                                               basis[:, nb % SLOTS, g, s2], start=(s == 0), stop=(s == 3),
                                               tile_position=(0, 32 * g))
                        if half == 0:
                            mm.then_inc(basis_used, 1)
                        nb += 1
                elif kind == "xT":
                    _, layer, m = name
                    if layer == 0:
                        pe.wait_ge(x1_ready, m + 1)
                        src = x1
                    else:
                        drained_by(pe, ("out", 0, m))
                        src = h1
                    for k in range(KT):
                        mm = pe.transpose(bank[:, k * P:(k + 1) * P], src[:, m, k * P:(k + 1) * P], ident[:])
                elif kind == "gate":
                    drained_by(pe, ("xT", name[1], NT - 1))
                    for m in range(NT):
                        for k in range(KT):
                            mm = pe.matmul(bank[:, 2 * m:2 * m + 2], RT[:, k, m * P:(m + 1) * P],
                                           gw[:, name[1], k], start=(k == 0), stop=(k == KT - 1))
                elif kind == "Z":
                    _, layer, r, i, h = name
                    if (r, i, h) == (0, 0, 0):
                        pe.wait_ge(y_ready[layer], NT * REL)
                    for m in range(NT):
                        mm = pe.matmul(bank[:, 0:HALF], y_sb[:, m, r, i * P:(i + 1) * P],
                                       CT[:, m, r * NP + h * HALF:r * NP + (h + 1) * HALF],
                                       start=(m == 0), stop=(m == NT - 1))
                elif kind == "out":
                    _, layer, m = name
                    if m == 0:
                        drained_by(pe, ("Z", layer, 1, KT - 1, 0))
                        drained_by(pe, ("Z", layer, 1, KT - 1, 1))
                        pe.wait_ge(w_in, 16 * REL * KT * (layer + 1))
                        pe.wait_ge(root_in[layer], 16)
                    pe.matmul(bank, ones[0:1, :], rbias[0:1, layer], start=True, stop=False)
                    for k in range(KT):
                        pe.matmul(bank, RT[:, k, m * P:(m + 1) * P], root[layer][:, k], start=False, stop=False)
                    for q in range(2 * KT):
                        mm = pe.matmul(bank, ZT[:, q, m * P:(m + 1) * P], w_sb[:, q // KT, q % KT],
                                       start=False, stop=(q == 2 * KT - 1))
                mm.then_inc(bank_full, 1)


def kernel(**inputs):
    import concourse.bacc as bacc
    from concourse.bass_utils import run_bass_kernel_spmd

    a = {k: np.asarray(v) for k, v in inputs.items()}
    f32 = np.float32

    def edge_columns(v, fill):
        return np.ascontiguousarray(np.concatenate([v, np.full(ET * P - E, fill, v.dtype)]).reshape(ET, P).T)

    def k_tiles(m):
        return np.ascontiguousarray(m.reshape(-1, P, m.shape[1]).transpose(1, 0, 2))

    x = np.concatenate([a["x"], np.zeros((NP - N, H), f32)])
    ea = np.concatenate([a["edge_attr_128"], np.zeros((ET * P - E, ED), f32)])
    W1 = a["L0_gnn_W1"]
    arrays = {
        "src": edge_columns(a["src"], 0),
        "dst": edge_columns(a["dst"], -1),
        "typ": edge_columns(a["edge_type_2"], 0),
        "x": k_tiles(x),
        "xT": k_tiles(x.T),
        "eaT": np.ascontiguousarray(ea.T),
        "W1aT": k_tiles(W1[:, :H].T),
        "W1bT": np.ascontiguousarray(W1[:, H:].T),
        "W2T": k_tiles(a["L0_gnn_W2"].T),
        "WihT": k_tiles(a["L0_gnn_W_ih"].T),
        "WhhT": k_tiles(a["L0_gnn_W_hh"].T),
        "rows": np.concatenate([a["L0_gnn_b1"], a["L0_gnn_b2"]])[None],
        "gbias": np.stack([a["L0_gnn_b_ih"], a["L0_gnn_b_hh"]]),
        "rbias": np.stack([a["L1_gnn_bias1"], a["L1_gnn_bias2"]])[None],
        "gamma": a["L0_gnn_gamma"][None],
        "beta": a["L0_gnn_beta"][None],
        "mean": a["L0_gnn_run_mean"][None],
        "var": a["L0_gnn_run_var"][None],
        "basis1": a["L1_gnn_basis1"],
        "basis2": a["L1_gnn_basis2"],
        "root1": k_tiles(a["L1_gnn_root1"]),
        "root2": k_tiles(a["L1_gnn_root2"]),
        "att": np.ascontiguousarray(np.repeat(np.stack([a["L1_gnn_att1"], a["L1_gnn_att2"]]).transpose(2, 0, 1),
                                              QTR, axis=0)),
        "gw": np.ascontiguousarray(np.stack([a["L1_gnn_gate_w1"], a["L1_gnn_gate_w2"]])[..., 0]
                                   .reshape(2, REL, KT, P).transpose(3, 0, 2, 1)),
        "iota": np.tile(np.arange(RN, dtype=np.float16), (P, 1)),
        "ident": np.eye(P, dtype=f32),
        "pick": np.stack([np.zeros(P, f32), np.ones(P, f32)]),
        "maskc": np.tile(np.eye(QTR, dtype=f32), (BASES, 1)),
    }
    nc = bacc.Bacc("TRN2", target_bir_lowering=False, num_devices=1)
    ins = {f"in_{k}": np.ascontiguousarray(v) for k, v in arrays.items()}
    t = {k[3:]: nc.dram_tensor(k, v.shape, mybir.dt.from_np(v.dtype), kind="ExternalInput").ap()
         for k, v in ins.items()}
    t["basis"] = [t["basis1"], t["basis2"]]
    t["root"] = [t["root1"], t["root2"]]
    t["bn"] = [t["gamma"], t["beta"], t["mean"], t["var"]]
    t["u"] = nc.dram_tensor("u_rows", (NP, H), F32, kind="Internal").ap()
    w = [nc.dram_tensor(f"w_layer{i}", (WT, P, H), F32, kind="Internal").ap() for i in range(2)]
    t["w"] = w
    t["out"] = nc.dram_tensor("out_rows", (NP, H), F32, kind="ExternalOutput").ap()
    gnn_kernel(nc, t)
    r = run_bass_kernel_spmd(nc, [ins], core_ids=[0])
    return r.results[0]["out_rows"][:N]
```

```python
from contextlib import ExitStack

import numpy as np

import concourse.bass as bass
from concourse import mybir
from concourse.alu_op_type import AluOpType as ALU

ACT = mybir.ActivationFunctionType
AX = mybir.AxisListType
F32 = mybir.dt.float32
F32R = mybir.dt.float32r
F16 = mybir.dt.float16
BF16 = mybir.dt.bfloat16
I32 = mybir.dt.int32

P = 128
N = 625
NT = 5
NP = NT * P
E = 10000
ET = 80
H = 512
KT = H // P
ED = 128
BASES = 30
REL = 2
UNIT = 4
UNITS = ET // UNIT
TURN = 4
TURNS = UNITS // TURN
EA_BANKS = (5, 7, 6, 6)
EARLY_BANK = 3
QTR = 4
BK = BASES * QTR
CONSTS = 6
WT = H // (QTR * 16)
HALF = NP // 2
RN = REL * NP
EXACT = 4096
PACK = 8
GPACK = 32
BN_EPS = 1e-5
LN_EPS = 1e-5
W_AFTER_M = ((1, 1), (1, 4), (0, 3))
SLOTS = 2


def plan_jobs():
    jobs = [(("RT", n), "AV"[n % 2]) for n in range(NT)]
    jobs += [(("cnt", 0), "V"), (("cnt", 1), "V")]
    jobs += [(("agg", o, h), "AV"[h]) for o in range(KT) for h in range(2)]
    composed = [(("w", layer, tile), "V") for layer in range(2) for tile in range(WT)]
    composed.pop(0)
    jobs.insert(0, composed.pop(0))

    for n in range(NT):
        jobs.append((("r", n), "A"))
        if n < NT - 1:
            jobs.append(composed.pop(0))
        jobs.append((("z", n), "A"))
        if n == NT - 1:
            jobs.append(composed.pop(0))
        jobs.append((("hn", n), "V"))
        if n < NT - 1:
            jobs.append(composed.pop(0))
        jobs.append((("in", n), "V"))
    jobs += [(("xT", 0, n), "V") for n in range(NT - 2)]
    for layer in range(2):
        for r in (1, 0):
            for n in range(NT):
                if (layer, r, n) == (0, 1, NT - 2):
                    jobs += [(("xT", 0, n), "V"), (("xT", 0, n + 1), "V")]
                jobs.append((("M", layer, n, r), "V"))
                if layer == 0 and (r, n) in W_AFTER_M:
                    jobs.append(composed.pop(0))
        for n in range(NT):
            jobs.append((("out", layer, n), "AV"[layer]))
            if layer == 0:
                if n >= 1:
                    jobs.append((("xT", 1, n - 1), "V"))
                if composed:
                    jobs.append(composed.pop(0))
        if layer == 0:
            jobs.append((("xT", 1, NT - 1), "V"))
    return jobs


class Jobs:

    def __init__(self):
        self.list = plan_jobs()
        self.at = {name: n for n, (name, _) in enumerate(self.list)}
        self.drains = {}
        count = {"A": 0, "V": 0}
        for name, e in self.list:
            count[e] += 1
            self.drains[name] = (e, count[e])
        split = [name for name, _ in self.list if name[0] in ("w", "xT", "M")]
        self.upper = {name: n + 2 for n, name in enumerate(split)}

    def bank(self, name):
        return (self.at[name] + 7) % 8


def gnn_kernel(nc, t):
    jobs = Jobs()
    ctx = ExitStack()
    with ctx:
        def sb(name, shape, dt=F32):
            return ctx.enter_context(nc.sbuf_tensor(name, shape, dt))

        def sem(name):
            return ctx.enter_context(nc.semaphore(name))

        x_sb = sb("x_sb", [P, NT, H])
        with nc.sbuf_tensor("xT", [P, KT, NP], F32) as xT:
            pass
        root_hi = sb("root_hi", [P, KT * NP], F32R)[:, 0:KT * H].rearrange("p (k n) -> p k n", k=KT)
        x1 = sb("x1", [P, NT, H])
        with nc.sbuf_tensor("CT", [P, NT, RN], F32) as CT:
            pass
        CT_r = sb("CT_r", [P, NT, RN], F32R)
        basis = sb("basis", [BK, SLOTS, QTR, 2, H])
        with nc.sbuf_tensor("R", [P, NT * H], F32) as R:
            pass
        xT_lo = sb("xT_lo", [P, KT, NP], F32R)
        with nc.sbuf_tensor("RT", [P, KT, NP], F32) as RT:
            pass
        xT_hi = sb("xT_hi", [P, KT, NP], F32R)
        with nc.sbuf_tensor("W2T", [P, KT, H], F32) as W2T:
            pass
        root_lo = sb("root_lo", [P, KT, H], F32R)
        bn = sb("bn", [P, 2, H])
        ev = sb("ev", [P, 2, H], F32R)
        with nc.sbuf_tensor("X", [P, 14 * 1024], F32) as X:
            pass
        with (nc.sbuf_tensor("x_kept", [P, 4608], F32),
              nc.sbuf_tensor("rhi", [P, 2, UNIT, H], F32R) as rhi,
              nc.sbuf_tensor("rlo", [P, 2, UNIT, H], F32R) as rlo,
              nc.sbuf_tensor("oh", [P, 2, UNIT, P], F32R) as oh):
            pass
        Mhi = sb("Mhi", [P, NT, REL, H], F32R)
        Mlo = sb("Mlo", [P, NT, REL, H], F32R)
        w_lo = sb("w_lo", [P, REL, KT, H], F32R)
        with nc.sbuf_tensor("bn_rows", [P, KT, H], F32) as bn_rows:
            pass
        w_hi = sb("w_hi", [P, REL, KT, H], F32R)
        work = X[:, 12032:14032]
        iota = sb("iota", [P, RN], F16)
        ident = sb("ident", [P, P])
        esrc = sb("esrc", [P, ET], I32)
        edst = sb("edst", [P, ET], I32)
        etyp = sb("etyp", [P, ET], I32)
        dstf = sb("dstf", [P, ET])
        keyf = sb("keyf", [P, ET])
        srcf = x1[:, 3, P:P + ET]
        drow = x1[0:ET, 3, 0:P].bitcast(I32)
        span = sb("span", [ET, 2])
        tab = work[0:1, 0:3 * NT * ET].rearrange("p (q j t) -> p q j t", q=3, j=NT)
        has = work[0:1, 1200:1600].rearrange("p (j t) -> p j t", j=NT)
        has2 = work[0:1, 1600:2000].rearrange("p (j t) -> p j t", j=NT)
        sprow = sb("sprow", [1, 2, ET])
        uspan = sb("uspan", [1, 3, UNITS])
        winf = sb("winf", [1, UNITS + 1])
        winp = sb("winp", [1, 2, UNITS])
        wins = sb("wins", [1, UNITS], I32)
        gspf = sb("gspf", [1, 4, NT])
        flagf = sb("flagf", [1, 1])
        flag = sb("flag", [1, 1], I32)
        gspan = sb("gspan", [1, 3, NT], I32)
        rows = bn[0:1, 0]
        gate_rows = [[RT[:, :, (NT - 2 + r) * P:(NT - 1 + r) * P] for r in range(REL)],
                     [bn[:, r].rearrange("p (k n) -> p k n", k=KT) for r in range(REL)]]
        dump = iota[:].bitcast(F32)[:, 0:H].rearrange("p (k n) -> p k n", k=KT)
        bias = sb("bias", [P, 2, H], F32R)
        bias_raw = x1[:, 0:2]
        picks = sb("picks", [P, 2, P], F32R)
        picks_raw = x1[:, 2, 0:2 * P].rearrange("p (q n) -> p q n", q=2)
        halves = sb("halves", [P, 2])
        zer = RT[:, 0, 0:H // 2].bitcast(BF16)
        cnt = sb("cnt", [P, NT])
        cntrow = iota[0:1, :].bitcast(F32)
        maskc = sb("maskc", [BK, QTR])
        att = sb("att", [BK, 2, REL])
        sel = sb("sel", [BK, 2, 4, 32])
        gate = sb("gate", [P, 2, 2 * NT])
        stat = sb("stat", [P, 2, 6])
        mv = sb("mv", [P, 2, 2])
        sd = sb("sd", [P, 2, 2])
        epst = sb("epst", [P, 1])

        ps = ctx.enter_context(nc.psum_tensor("ps", [P, 8, 512], F32))
        flat = ps[:].rearrange("p b n -> p (b n)")

        eaT = X[:, 0:1024].rearrange("p (s n) -> p s n", s=2)
        gat = X[:, 1024:3072].rearrange("p (s n) -> p s n", s=UNIT)
        pre = x1[:, 0:UNIT]
        W1bT = X[:, 4096:4608]
        W1aT = X[:, 4608:6656].rearrange("p (k n) -> p k n", k=KT)
        u_sb = X[:, 6656:9216].rearrange("p (k n) -> p k n", k=NT)
        ohs = X[:, 9216:11776].bitcast(BF16).rearrange("p (s n) -> p s n", s=UNIT)
        ohd = X[:, 11776:12032].bitcast(BF16).rearrange("p (s n) -> p s n", s=UNIT)
        drowf = X[0:ET, 14032:14160]
        WihT = X[:, 0:6144].rearrange("p (k n) -> p k n", k=KT)
        WhhT = X[:, 6144:12288].rearrange("p (k n) -> p k n", k=KT)
        gru = W2T
        aggT = R[:, :].rearrange("p (k n) -> p k n", k=KT)
        R_v = R[:, :].rearrange("p (m n) -> p m n", m=NT)
        h1 = x_sb

        idx_in = sem("idx_in")
        span_in = sem("span_in")
        const_in = sem("const_in")
        w1a_in = sem("w1a_in")
        xt_in = [sem(f"xt_in{n}") for n in range(NT)]
        x_in = sem("x_in")
        w1b_in = sem("w1b_in")
        rows_in = sem("rows_in")
        w2_in = sem("w2_in")
        bias_in = sem("bias_in")
        bias_ready = sem("bias_ready")
        gru_in = sem("gru_in")
        ea_in = [sem(f"ea_in{i}") for i in range(2)]
        gat_in = [sem(f"gat_in{i}") for i in range(4)]
        basis_in = [sem(f"basis_in{i}") for i in range(SLOTS)]
        root_in = sem("root_in")
        root_hi_ready = sem("root_hi_ready")
        root_ready = sem("root_ready")
        gate_in = [sem("gate_in0"), sem("gate_in1")]
        gate_sums = sem("gate_sums")
        gates_ready = sem("gates_ready")
        w_hi_in = sem("w_hi_in")
        w_lo_in = [sem("w_lo_in0"), sem("w_lo_in1")]
        w_out = sem("w_out")
        u_out = sem("u_out")
        y_out = sem("y_out")
        dve_step = sem("dve_step")
        setup_ready = sem("setup_ready")
        sel_ready = sem("sel_ready")
        span_ready = sem("span_ready")
        span_row = sem("span_row")
        spans_in_sbuf = sem("spans_in_sbuf")
        hot_ready = sem("hot_ready")
        hot_free = sem("hot_free")
        ct_acc = sem("ct_acc")
        ct_drained = sem("ct_drained")
        u_acc = sem("u_acc")
        u_drained = sem("u_drained")
        ea_done = sem("ea_done")
        pre_ready = sem("pre_ready")
        hi_ready = sem("hi_ready")
        lo_ready = sem("lo_ready")
        oh_ready = sem("oh_ready")
        oh_free = sem("oh_free")
        sums_done = sem("sums_done")
        r_acc = sem("r_acc")
        var_ready = sem("var_ready")
        std_ready = sem("std_ready")
        r_drained = sem("r_drained")
        bank_full = sem("bank_full")
        drained = {"A": sem("act_drained"), "V": sem("dve_drained")}
        basis_used = sem("basis_used")
        n_ready = sem("n_ready")
        x1_sum = sem("x1_sum")
        sd_ready = sem("sd_ready")
        x1_ready = sem("x1_ready")
        early_full = sem("early_full")
        early_drained = sem("early_drained")
        upper_ready = sem("upper_ready")
        flag_ready = sem("flag_ready")
        ct_rounded = sem("ct_rounded")
        out_ready = sem("out_ready")

        def drained_by(eng, name):
            e, n = jobs.drains[name]
            eng.wait_ge(drained[e], n)

        def full(eng, name):
            eng.wait_ge(bank_full, jobs.at[name] + 1)

        def load_basis(eng, c):
            layer, tile, half = c // (2 * WT), c // 2 % WT, c % 2
            if c >= 2 * SLOTS:
                old = c - SLOTS
                if old % 2:
                    full(eng, ("w", old // (2 * WT), old // 2 % WT))
                else:
                    eng.wait_ge(basis_used, old // 2 + 1)
            src = t["basis"][layer].rearrange(
                "b (c w g h s) o -> (b c) w g h (s o)", c=QTR, w=WT, g=4, h=2)[:, tile, :, half]
            eng.dma_start(basis[:, c % SLOTS].rearrange("p g s o -> p g (s o)"),
                         src).then_inc(basis_in[c % SLOTS], 16)

        def windows(eng, tile):
            v = eng.value_load(wins[0:1, bass.ds(tile, 1)], min_val=0, max_val=PACK * PACK * (NT + 1) * UNITS)
            first = (v % PACK).with_bounds(min_val=0, max_val=NT - 1)
            end = (v // PACK % PACK).with_bounds(min_val=1, max_val=NT)
            return [first, end, v // (PACK * PACK)]

        def unit_span(eng, j):
            v = eng.value_load(gspan[0:1, 2, j:j + 1], min_val=0, max_val=GPACK * GPACK * (NT + 2) * UNITS)
            first = (v % GPACK).with_bounds(min_val=0, max_val=UNITS - 1)
            end = (v // GPACK % GPACK).with_bounds(min_val=1, max_val=UNITS)
            return [first, end, v // (GPACK * GPACK)]

        block = ctx.enter_context(nc.Block())

        @block.sync
        def _(sp):
            for a, b in ((drow[:], t["dstrow"]), (tab, t["tab"]), (ident[:], t["ident"])):
                sp.dma_start(a, b).then_inc(span_in, 16)
            for a, b in ((esrc, t["src"]), (edst, t["dst"]), (etyp, t["typ"]), (iota, t["iota"])):
                sp.dma_start(a[:], b).then_inc(idx_in, 16)
            for a, b in ((bias_raw, t["bias"]), (picks_raw, t["picks"]), (halves[:], t["halves"])):
                sp.dma_start(a, b).then_inc(bias_in, 16)
            sp.dma_start(rows, t["rows"]).then_inc(rows_in, 16)
            sp.dma_start(W1aT, t["W1aT"]).then_inc(w1a_in, 16)
            for n in range(NT):
                sp.dma_start(xT[:, :, n * P:(n + 1) * P], t["xT"][:, :, n * P:(n + 1) * P]
                             ).then_inc(xt_in[n], 16)
            for a, b in ((maskc, t["maskc"]), (att, t["att"])):
                sp.dma_start(a[:], b).then_inc(const_in, 16)
            for i, a in enumerate(t["bn"]):
                sp.dma_start(bn_rows[:, i], a.broadcast_to([P, H])).then_inc(const_in, 16)
            sp.dma_start(W1bT, t["W1bT"]).then_inc(w1b_in, 16)
            sp.dma_start(x_sb[:], t["x"]).then_inc(x_in, 16)
            sp.dma_start(W2T[:], t["W2T"]).then_inc(w2_in, 16)

            def load_gate_rows(layer):
                for r in range(REL):
                    src = t["gw"][layer][:, r].rearrange("a (k n) -> a k n", k=KT)
                    sp.dma_start(gate_rows[layer][r], src.broadcast_to([P, KT, P])).then_inc(gate_in[layer], 16)

            for c in range(SLOTS):
                load_basis(sp, c)
            for n in range(NT):
                sp.wait_ge(u_drained, n + 1)
                sp.dma_start(t["u"][n * P:(n + 1) * P, :], u_sb[:, n]).then_inc(u_out, 16)

            def load_attributes(it):
                for s in range(2):
                    sp.wait_ge(ea_done, it * (2 * UNIT) + UNIT * (s + 1))
                    sp.dma_start(eaT[:, s], t["eaT"][:, bass.ds(it * (2 * UNIT * P) + s * H, H)]
                                 ).then_inc(ea_in[s], 16)

            assert SLOTS == 2
            plain = UNITS // 2 - SLOTS * 4
            with sp.Fori(0, plain) as it:
                load_attributes(it)
            sp.wait_ge(early_full, 1)
            for half in range(SLOTS):
                rows_of_half = t["basis"][0].rearrange(
                    "b (c w g h s) o -> (b c) w g h (s o)", c=QTR, w=WT, g=4, h=2)[:, 1, :, half]
                slot = basis[:, half].rearrange("p g s o -> p g (s o)")
                with sp.Fori(plain + 4 * half, plain + 4 * (half + 1)) as it:
                    load_attributes(it)
                    g = it - (plain + 4 * half)
                    sp.dma_start(slot[:, bass.ds(g, 1)], rows_of_half[:, bass.ds(g, 1)]
                                 ).then_inc(basis_in[half], 16)
            sp.wait_ge(r_drained, NT)
            sp.dma_start(WihT, t["WihT"]).then_inc(gru_in, 16)
            sp.dma_start(WhhT, t["WhhT"]).then_inc(gru_in, 16)

            nb = 2 * SLOTS
            for name, _ in jobs.list:
                if name[0] == "w":
                    _, layer, tile = name
                    for _ in range(2):
                        if nb < 2 * WT * 2:
                            load_basis(sp, nb)
                            nb += 1
                    drained_by(sp, name)
                    sp.dma_start(t["w"][layer][tile], ev[:].bitcast(F32)).then_inc(w_out, 16)
                if name == ("agg", KT - 1, 1):
                    full(sp, name)
                    load_gate_rows(0)
                if name == ("in", NT - 1):
                    sp.wait_ge(x1_ready, NT)
                    load_gate_rows(1)
                if name == ("M", 0, NT - 1, 1):
                    sp.dma_start(W2T[:], t["root"][0]).then_inc(root_in, 16)
                if name == ("out", 0, NT - 1):
                    full(sp, name)
                    sp.dma_start(W2T[:], t["root"][1]).then_inc(root_in, 16)
            for n in range(NT):
                sp.wait_ge(out_ready, n + 1)
                sp.dma_start(t["out"][n * P:(n + 1) * P, :], h1[:, n]).then_inc(y_out, 16)
            sp.wait_ge(y_out, 16 * NT)
            sp.wait_ge(u_out, 16 * NT)

        @block.gpsimd
        def _(pool):
            pool.wait_ge(idx_in, 64)
            pool.wait_ge(u_out, 16 * NT)
            for e in range(ET):
                pool.wait_ge(pre_ready, e + 1)
                nc.gpsimd.indirect_dma_start(
                    gat[:, e % 4], None, t["u"][:, :],
                    bass.IndirectOffsetOnAxis(ap=esrc[:, e:e + 1], axis=0)).then_inc(gat_in[e % 4], 16)

            def load_w(layer, r, part, into, done):
                for k in range(KT):
                    src = t["w"][layer].rearrange("w (g r c s) h o -> r c h (w g) s o", g=4, r=REL, c=QTR)
                    nc.gpsimd.dma_start(into[:, r, k], src[r, k, part]).then_inc(done, 16)

            pool.wait_ge(w_out, 16 * WT)
            pool.wait_ge(x1_sum, 1)
            for r in range(REL):
                load_w(0, r, 0, w_hi, w_hi_in)
            load_w(0, 1, 1, w_lo, w_lo_in[1])
            full(pool, ("in", NT - 1))
            load_w(0, 0, 1, w_lo, w_lo_in[0])
            pool.wait_ge(w_out, 2 * 16 * WT)
            full(pool, ("M", 0, NT - 1, 0))
            for r in (1, 0):
                load_w(1, r, 0, w_hi, w_hi_in)
                load_w(1, r, 1, w_lo, w_lo_in[r])

        @block.scalar
        def _(act):
            def drain_u(n):
                act.wait_ge(u_acc, n + 1)
                nc.scalar.copy(u_sb[:, n], ps[:, 6 + n % 2]).then_inc(u_drained, 1)

            drain_u(0)
            drain_u(1)
            for j in range(NT):
                act.wait_ge(ct_acc, j + 1)
                b = 3 * (j % 2) * 512
                nc.scalar.activation(CT[:, j], flat[:, b:b + RN], ACT.Copy, accum_out=cnt[:, j:j + 1]
                                     ).then_inc(ct_drained, 1)
                if j + 2 < NT:
                    drain_u(j + 2)
            act.wait_ge(early_full, 1)
            nc.scalar.copy(ev[:, 0], ps[:, EARLY_BANK]).then_inc(upper_ready, 1)
            act.wait_ge(early_drained, 1)
            act.dma_start(t["w"][0][0], ev[:].bitcast(F32)).then_inc(w_out, 16)
            with act.Fori(0, UNITS // 2) as it:
                for h in range(2):
                    act.wait_ge(sums_done, it * 2 + h + 1)
                    for s in range(UNIT):
                        act.wait_ge(pre_ready, it * (2 * UNIT) + h * UNIT + s + 5)
                        nc.scalar.activation(rhi[:, h, s], pre[:, s], ACT.Relu).then_inc(hi_ready, 1)
            for n in range(NT):
                act.wait_ge(r_acc, 1)
                nc.scalar.copy(R_v[:, n], ps[:, n]).then_inc(r_drained, 1)
            def deviation(turn):
                act.wait_ge(x1_sum, turn + 1)
                nc.scalar.activation(sd[:, 0, 0:1], mv[:, 0, 1:2], ACT.Sqrt,
                                     bias=epst[:, 0:1]).then_inc(sd_ready, 1)

            nw = 1
            for name, e in jobs.list:
                kind = name[0]
                bank = ps[:, jobs.bank(name)]
                if e == "A":
                    full(act, name)
                    if kind == "RT":
                        ins = nc.scalar.copy(RT[:, :, name[1] * P:(name[1] + 1) * P],
                                             bank.rearrange("p (k n) -> p k n", k=KT))
                    elif kind == "agg":
                        ins = nc.scalar.copy(aggT[:, name[1], 0:HALF], bank[:, 0:HALF])
                    elif kind in "rz":
                        if name[1] >= 1:
                            act.wait_ge(x1_sum, name[1])
                        ins = nc.scalar.activation(gru[:, "rz".index(kind)], bank, ACT.Sigmoid)
                    elif kind == "out":
                        ins = nc.scalar.activation(h1[:, name[2]], bank, ACT.Relu)
                    ins.then_inc(drained["A"], 1)
                if name == ("agg", KT - 1, 1):
                    act.wait_ge(var_ready, 1)
                    nc.scalar.activation(bn[:, 0], bn[:, 1], ACT.Sqrt).then_inc(std_ready, 1)
                    act.wait_ge(flag_ready, 1)
                    many = act.value_load(flag[0:1, 0:1], min_val=0, max_val=1)
                    with act.If(many < 1):
                        for n in range(NT):
                            nc.scalar.copy(CT_r[:, n], CT[:, n]).then_inc(ct_rounded, 1)
                    with act.If(many > 0):
                        act.nop().then_inc(ct_rounded, NT)
                if kind in ("w", "xT", "M"):
                    full(act, name)
                    if kind == "w":
                        act.wait_ge(w_out, 16 * nw)
                        nw += 1
                        ins = nc.scalar.copy(ev[:, 0], bank)
                    elif kind == "xT":
                        ins = nc.scalar.copy(xT_hi[:, :, name[2] * P:(name[2] + 1) * P],
                                             bank.rearrange("p (k n) -> p k n", k=KT))
                    else:
                        _, layer, m, r = name
                        act.wait_ge(gates_ready, 1 if layer == 0 else m + 2)
                        if layer == 1:
                            full(act, ("out", 0, NT - 1))
                        ins = nc.scalar.activation(Mhi[:, m, r], bank, ACT.Copy,
                                                   scale=gate[:, layer, 2 * m + r:2 * m + r + 1])
                    ins.then_inc(upper_ready, 1)
                if name == ("xT", 0, NT - 3):
                    deviation(NT - 1)
                    act.wait_ge(gate_sums, NT)
                    nc.scalar.activation(gate[:, 0], gate[:, 0], ACT.Sigmoid).then_inc(gates_ready, 1)
                if kind == "xT" and name[1] == 1:
                    m = name[2]
                    act.wait_ge(gate_sums, NT + m + 1)
                    nc.scalar.activation(gate[:, 1, 2 * m:2 * m + 2], gate[:, 1, 2 * m:2 * m + 2],
                                         ACT.Sigmoid).then_inc(gates_ready, 1)
                if name in (("M", 0, 1, 0), ("M", 1, NT - 1, 1)):
                    act.wait_ge(root_in, 16 * (name[1] + 1))
                    nc.scalar.copy(root_hi, W2T[:]).then_inc(root_hi_ready, 1)
                if kind == "in":
                    drained_by(act, name)
                    nc.scalar.activation(gru[:, 3], gru[:, 2], ACT.Tanh).then_inc(n_ready, 1)
                    if name[1] < NT - 1:
                        deviation(name[1])
                if kind == "out" and name[1] == 1:
                    deviation(NT + name[2])

        @block.vector
        def _(dve):
            steps = [0]

            def step(ins):
                steps[0] += 1
                ins.then_inc(dve_step, 1)
                dve.wait_ge(dve_step, steps[0])

            dve.nop().then_inc(hot_ready, UNITS * UNIT)
            dve.nop().then_inc(pre_ready, 4)
            dve.nop().then_inc(lo_ready, UNIT)
            dve.nop().then_inc(oh_ready, NT * UNIT)
            dve.memset(epst[:], LN_EPS)
            dve.memset(sel[:], 0.0)
            step(dve.memset(winf[:, 0:1], 0.0))
            dve.memset(zer, 0.0).then_inc(setup_ready, 1)
            dve.wait_ge(span_in, 48)
            step(dve.tensor_scalar(drow[:], drow[:], P.bit_length() - 1, None, ALU.arith_shift_right))
            step(dve.tensor_copy(drowf, drow[:]))
            dve.tensor_reduce(span[:, 0:1], drowf, AX.X, ALU.min)
            dve.tensor_reduce(span[:, 1:2], drowf, AX.X, ALU.max).then_inc(span_ready, 1)
            dve.wait_ge(idx_in, 64)
            dve.tensor_copy(srcf[:], esrc[:])
            dve.tensor_copy(dstf[:], edst[:])
            step(dve.tensor_copy(keyf[:], etyp[:]))
            step(dve.tensor_scalar(keyf[:], keyf[:], 0.0, float(NP), ALU.not_equal, ALU.mult))
            step(dve.tensor_tensor(keyf[:], keyf[:], srcf[:], ALU.add))
            dve.wait_ge(bias_in, 48)
            dve.tensor_copy(picks[:], picks_raw)
            step(dve.tensor_copy(bias[:], bias_raw))
            step(dve.tensor_scalar(bias_raw, bias_raw, halves[:, 0:1], None, ALU.mult))
            nc.vector.scalar_tensor_tensor(out=bias[:], in0=bias[:].bitcast(F32), scalar=halves[:, 1:2],
                                           in1=bias_raw, op0=ALU.mult, op1=ALU.add).then_inc(bias_ready, 1)
            dve.wait_ge(span_row, 1)
            step(dve.tensor_copy(sprow[:, 0:2], ps[0:1, 4, 0:2 * ET].rearrange("p (q t) -> p q t", q=2)))
            by_unit = sprow[:, 0:2].rearrange("p q (u s) -> p q u s", s=UNIT)
            dve.tensor_reduce(uspan[:, 0], by_unit[:, 0], AX.X, ALU.min)
            step(dve.tensor_reduce(uspan[:, 1], by_unit[:, 1], AX.X, ALU.max))
            step(nc.vector.scalar_tensor_tensor(out=uspan[:, 2], in0=uspan[:, 1], scalar=1.0,
                                                in1=uspan[:, 0], op0=ALU.add, op1=ALU.subtract))
            step(dve.tensor_tensor_scan(winf[:, 1:UNITS + 1], uspan[:, 2], uspan[:, 2], 0.0, ALU.add, ALU.bypass))
            dve.tensor_scalar(winp[:, 0], uspan[:, 1], 1.0, None, ALU.add)
            step(dve.tensor_tensor(winp[:, 1], winf[:, 0:UNITS], uspan[:, 0], ALU.subtract))
            step(dve.tensor_scalar(winp[:, 1], winp[:, 1], float(NT), float(PACK), ALU.add, ALU.mult))
            step(dve.tensor_tensor(winp[:, 1], winp[:, 1], winp[:, 0], ALU.add))
            step(dve.tensor_scalar(winp[:, 1], winp[:, 1], float(PACK), None, ALU.mult))
            dve.tensor_tensor(wins[:], winp[:, 1], uspan[:, 0], ALU.add)
            rows_of = [sprow[:, q:q + 1, :].broadcast_to([1, NT, ET]) for q in range(2)]
            dve.tensor_tensor(has, rows_of[0], tab[:, 0], ALU.is_le)
            step(dve.tensor_tensor(has2, rows_of[1], tab[:, 0], ALU.is_ge))
            step(dve.tensor_tensor(has, has, has2, ALU.mult))
            step(dve.tensor_tensor(has2, has, tab[:, 2], ALU.mult))
            dve.tensor_reduce(gspf[:, 0], has2, AX.X, ALU.max)
            step(dve.tensor_tensor(has, has, tab[:, 1], ALU.mult))
            step(dve.tensor_reduce(gspf[:, 1], has, AX.X, ALU.max))
            step(dve.tensor_scalar(gspf[:, 0], gspf[:, 0], -1.0, float(ET), ALU.mult, ALU.add))
            step(dve.tensor_scalar(gspf[:, 0], gspf[:, 0], float(ET - 1), None, ALU.min))
            step(nc.vector.scalar_tensor_tensor(out=gspf[:, 1], in0=gspf[:, 0], scalar=1.0,
                                                in1=gspf[:, 1], op0=ALU.add, op1=ALU.max))
            step(dve.tensor_scalar(gspf[:, 1], gspf[:, 1], float(UNIT - 1), None, ALU.add))
            step(dve.tensor_copy(gspan[:, 0:2], gspf[:, 0:2]))
            step(dve.tensor_scalar(gspan[:, 0:2], gspan[:, 0:2], UNIT.bit_length() - 1, None, ALU.arith_shift_right))
            step(dve.tensor_copy(gspf[:, 0:2], gspan[:, 0:2]))
            step(dve.tensor_tensor(gspf[:, 2], gspf[:, 1], gspf[:, 0], ALU.subtract))
            step(dve.tensor_tensor_scan(gspf[:, 3], gspf[:, 2], gspf[:, 2], 0.0, ALU.add, ALU.bypass))
            step(dve.tensor_tensor(gspf[:, 3], gspf[:, 3], gspf[:, 1], ALU.subtract))
            step(dve.tensor_scalar(gspf[:, 3], gspf[:, 3], float(UNITS), float(GPACK), ALU.add, ALU.mult))
            step(dve.tensor_tensor(gspf[:, 3], gspf[:, 3], gspf[:, 1], ALU.add))
            step(dve.tensor_scalar(gspf[:, 3], gspf[:, 3], float(GPACK), None, ALU.mult))
            dve.tensor_tensor(gspan[:, 2], gspf[:, 3], gspf[:, 0], ALU.add).then_inc(spans_in_sbuf, 1)
            dve.wait_ge(spans_in_sbuf, 1)
            ahead = unit_span(dve, 0)
            for j in range(NT):
                (first, end, before), ahead = ahead, unit_span(dve, (j + 1) % NT)
                with dve.Fori(first, end) as g:
                    for s in range(UNIT):
                        dve.wait_ge(hot_free, (g + before) * UNIT + s + 1)
                        dve.tensor_scalar(ohs[:, s], iota[:], keyf[:, bass.ds(g * UNIT + s, 1)], None,
                                          ALU.is_equal)
                        dve.tensor_scalar(ohd[:, s], iota[:, j * P:(j + 1) * P],
                                          dstf[:, bass.ds(g * UNIT + s, 1)], None,
                                          ALU.is_equal).then_inc(hot_ready, 1)
            dve.wait_ge(const_in, 16 * CONSTS)
            for layer in range(2):
                for r in range(REL):
                    for s in range(4):
                        last = dve.tensor_scalar(sel[:, layer, s, 16 * r + s:16 * r + 16:4], maskc[:],
                                                 att[:, layer, r:r + 1], None, ALU.mult)
            last.then_inc(sel_ready, 1)

            def add_rows(it, h, tiles):
                for s in tiles:
                    e = it * (TURN * UNIT) + h * UNIT + s
                    dve.wait_ge(ea_done, e + 2 * UNIT + 1)
                    dve.wait_ge(gat_in[s], (it * TURN + h + 1) * 16)
                    dve.wait_ge(lo_ready, e + 1)
                    dve.tensor_tensor(pre[:, s], ps[:, EA_BANKS[s]], gat[:, s], ALU.add
                                      ).then_inc(pre_ready, 1)

            def split(it, h, tiles):
                for s in tiles:
                    dve.wait_ge(hi_ready, it * (TURN * UNIT) + h * UNIT + s + 1)
                    nc.vector.scalar_tensor_tensor(
                        out=rlo[:, h % 2, s], in0=pre[:, s], scalar=0.0, in1=rhi[:, h % 2, s].bitcast(F32),
                        op0=ALU.max, op1=ALU.subtract).then_inc(lo_ready, 1)

            def one_hots(it, h, j, before):
                if before is None:
                    dve.wait_ge(sums_done, it * TURN + h + 1)
                for s in range(UNIT):
                    if before is not None:
                        dve.wait_ge(oh_free, (j + before) * UNIT + s + 1)
                    dve.tensor_scalar(oh[:, h % 2, s], iota[:, bass.ds(j * P, P)],
                                      dstf[:, bass.ds(it * (TURN * UNIT) + h * UNIT + s, 1)], None,
                                      ALU.is_equal).then_inc(oh_ready, 1)

            def unit(it, h, bounds, last=False):
                first, end, before = bounds
                one_hots(it, h, first, None)
                split(it, h, (0,))
                add_rows(it, h, (UNIT - 1,))
                split(it, h, (1, 2))
                ahead = None if h == TURN - 1 else windows(dve, it * TURN + h + 1)
                split(it, h, (3,))
                with dve.If(end > first + 1):
                    with dve.Fori(first + 1, end) as j:
                        one_hots(it, h, j, before)
                if not last:
                    add_rows(it, h + 1, range(UNIT - 1))
                return ahead

            def turn(it, last=False):
                bounds = windows(dve, it * TURN)
                for h in range(TURN):
                    bounds = unit(it, h, bounds, last and h == TURN - 1)

            add_rows(0, 0, range(UNIT - 1))
            dve.wait_ge(upper_ready, 1)
            dve.tensor_tensor(ev[:, 1], ps[:, EARLY_BANK], ev[:, 0].bitcast(F32), ALU.subtract
                              ).then_inc(early_drained, 1)
            with dve.Fori(0, TURNS - 1) as it:
                turn(it)
            turn(TURNS - 1, last=True)
            def layer_norm(rows_in, rows_out, turn, done):
                dve_bn = dve.bn_stats(stat[:, 0], rows_in)
                step(dve_bn)
                dve.bn_aggr(mv[:, 0], stat[:, 0]).then_inc(x1_sum, 1)
                dve.wait_ge(sd_ready, turn + 1)
                step(dve.reciprocal(sd[:, 0, 1:2], sd[:, 0, 0:1]))
                dve.tensor_scalar(rows_out, rows_in, mv[:, 0, 0:1], sd[:, 0, 1:2], ALU.subtract,
                                  ALU.mult).then_inc(done, 1)

            def update(n):
                drained_by(dve, ("in", n))
                dve.wait_ge(n_ready, n + 1)
                drained_by(dve, ("z", n))
                dve.wait_ge(x_in, 16)
                step(dve.tensor_tensor(gru[:, 2], x_sb[:, n], gru[:, 3], ALU.subtract))
                step(dve.tensor_tensor(gru[:, 2], gru[:, 1], gru[:, 2], ALU.mult))
                step(dve.tensor_tensor(gru[:, 3], gru[:, 2], gru[:, 3], ALU.add))
                step(dve.tensor_tensor(gru[:, 2], gru[:, 3], bn[:, 0], ALU.mult))
                step(dve.tensor_tensor(gru[:, 2], gru[:, 2], bn[:, 1], ALU.add))
                step(nc.vector.scalar_tensor_tensor(out=gru[:, 3], in0=x_sb[:, n], scalar=2.0,
                                                    in1=gru[:, 2], op0=ALU.mult, op1=ALU.add))
                layer_norm(gru[:, 3], x1[:, n], n, x1_ready)
                dve.wait_ge(x1_ready, n + 1)
                gate_products(0, n)

            def gate_products(layer, m):
                dve.wait_ge(gate_in[layer], 16 * REL)
                for r in range(REL):
                    last = nc.vector.scalar_tensor_tensor(
                        out=dump, in0=(x1, h1)[layer][:, m].rearrange("p (k n) -> p k n", k=KT),
                        scalar=1.0, in1=gate_rows[layer][r], op0=ALU.mult,
                        op1=ALU.mult, accum_out=gate[:, layer, 2 * m + r:2 * m + r + 1])
                    step(last)
                dve.nop().then_inc(gate_sums, 1)

            for name, e in jobs.list:
                kind = name[0]
                bank = ps[:, jobs.bank(name)]
                if e == "V":
                    full(dve, name)
                    if kind == "RT":
                        ins = dve.tensor_copy(RT[:, :, name[1] * P:(name[1] + 1) * P],
                                              bank.rearrange("p (k n) -> p k n", k=KT))
                    elif kind == "cnt":
                        a, b = ((0, 3), (3, NT))[name[1]]
                        ins = dve.tensor_copy(cntrow[0:1, a * P:b * P], bank[0:1, 0:(b - a) * P])
                    elif kind == "agg":
                        ins = dve.tensor_copy(aggT[:, name[1], HALF:NP], bank[:, 0:HALF])
                    elif kind == "hn":
                        drained_by(dve, ("r", name[1]))
                        ins = dve.tensor_tensor(gru[:, 2], bank, gru[:, 0], ALU.mult)
                    elif kind == "in":
                        drained_by(dve, ("hn", name[1]))
                        ins = dve.tensor_tensor(gru[:, 2], bank, gru[:, 2], ALU.add)
                    elif kind == "M":
                        _, layer, m, r = name
                        dve.wait_ge(upper_ready, jobs.upper[name])
                        ins = nc.vector.scalar_tensor_tensor(
                            out=Mlo[:, m, r], in0=bank, scalar=gate[:, layer, 2 * m + r:2 * m + r + 1],
                            in1=Mhi[:, m, r].bitcast(F32), op0=ALU.mult, op1=ALU.subtract)
                    elif kind == "w":
                        dve.wait_ge(upper_ready, jobs.upper[name])
                        ins = dve.tensor_tensor(ev[:, 1], bank, ev[:, 0].bitcast(F32), ALU.subtract)
                    elif kind == "xT":
                        cols = slice(name[2] * P, (name[2] + 1) * P)
                        dve.wait_ge(upper_ready, jobs.upper[name])
                        ins = dve.tensor_tensor(xT_lo[:, :, cols], bank.rearrange("p (k n) -> p k n", k=KT),
                                                xT_hi[:, :, cols].bitcast(F32), ALU.subtract)
                    elif kind == "out":
                        ins = dve.tensor_tensor(h1[:, name[2]], bank, x1[:, name[2]], ALU.add)
                    ins.then_inc(drained["V"], 1)
                if kind == "in" and name[1] < NT - 1:
                    update(name[1])
                if name == ("xT", 0, NT - 3):
                    update(NT - 1)
                if kind == "out" and name[1] == 0:
                    drained_by(dve, name)
                    gate_products(1, name[2])
                if name in (("M", 0, 1, 0), ("M", 1, NT - 1, 1)):
                    dve.wait_ge(root_hi_ready, name[1] + 1)
                    dve.tensor_tensor(root_lo[:], W2T[:], root_hi.bitcast(F32), ALU.subtract
                                      ).then_inc(root_ready, 1)
                if name == ("agg", KT - 1, 1):
                    step(dve.tensor_scalar(bn[:, 1], bn_rows[:, 3], BN_EPS, None, ALU.add))
                    dve.nop().then_inc(var_ready, 1)
                    dve.wait_ge(std_ready, 1)
                    step(dve.reciprocal(bn[:, 1], bn[:, 0]))
                    step(dve.tensor_tensor(bn[:, 0], bn[:, 1], bn_rows[:, 0], ALU.mult))
                    step(dve.tensor_tensor(bn[:, 1], bn[:, 0], bn_rows[:, 2], ALU.mult))
                    step(dve.tensor_tensor(bn[:, 1], bn_rows[:, 1], bn[:, 1], ALU.subtract))
                if name == ("cnt", 1):
                    drained_by(dve, name)
                    step(dve.tensor_reduce(flagf[:], cntrow[0:1, 0:NP], AX.X, ALU.max))
                    dve.tensor_scalar(flag[:], flagf[:], float(EXACT), None, ALU.is_gt).then_inc(flag_ready, 1)
                if kind == "out" and name[1] == 1:
                    drained_by(dve, name)
                    layer_norm(h1[:, name[2]], h1[:, name[2]], NT + name[2], out_ready)

        @block.tensor
        def _(pe):
            pe.nop().then_inc(ea_done, 2 * UNIT)
            pe.nop().then_inc(sums_done, 2)
            pe.nop().then_inc(hot_free, UNIT + UNITS * UNIT)
            pe.nop().then_inc(oh_free, UNIT + NT * UNIT)
            pe.wait_ge(setup_ready, 1)
            pe.wait_ge(span_ready, 1)
            for q in range(2):
                mm = pe.matmul(ps[0:1, 4, q * ET:(q + 1) * ET], span[:, q:q + 1], ident[0:ET, 0:ET],
                               start=True, stop=True)
            mm.then_inc(span_row, 1)

            def add_bias(bank, which, part, terms=4, pick=0, start=True):
                at = slice(32 * part, 32 * part + terms)
                return pe.matmul(bank, picks[at, pick], bias[at, which], start=start, stop=not start)

            def source_rows(n):
                pe.wait_ge(w1a_in, 16)
                pe.wait_ge(xt_in[n], 16)
                if n >= 2:
                    pe.wait_ge(u_drained, n - 1)
                bank = ps[:, 6 + n % 2]
                for k in range(KT):
                    pe.matmul(bank, xT[:, k, n * P:(n + 1) * P], W1aT[:, k], start=(k == 0), stop=False)
                if n == 0:
                    pe.wait_ge(bias_ready, 1)
                add_bias(bank, 1, 0, 2, start=False).then_inc(u_acc, 1)

            source_rows(0)
            source_rows(1)
            pe.wait_ge(spans_in_sbuf, 1)
            ahead = unit_span(pe, 0)
            for j in range(NT):
                if j >= 2:
                    pe.wait_ge(ct_drained, j - 1)
                banks = [ps[:, 3 * (j % 2) + c, 0:min(512, RN - 512 * c)] for c in range(3)]
                for bank in banks:
                    pe.matmul(bank, zer[:, 0:P], zer[:, 0:bank.shape[1]], start=True, stop=True)
                (first, end, before), ahead = ahead, unit_span(pe, (j + 1) % NT)
                with pe.Fori(first, end) as g:
                    for s in range(UNIT):
                        pe.wait_ge(hot_ready, (g + before) * UNIT + s + 1)
                        for c, bank in enumerate(banks):
                            mm = pe.matmul(bank, ohd[:, s], ohs[:, s, 512 * c:512 * c + bank.shape[1]],
                                           start=False, stop=True, skip_group_check=True)
                        mm.then_inc(hot_free, 1)
                pe.matmul(banks[2], zer[:, 0:P], zer[:, 0:banks[2].shape[1]], start=False, stop=True,
                          skip_group_check=True).then_inc(ct_acc, 1)
                if j + 2 < NT:
                    source_rows(j + 2)
            def attributes(it, h, s):
                if s == 0:
                    pe.wait_ge(ea_in[h % 2], (it * (TURN // 2) + h // 2 + 1) * 16)
                pe.wait_ge(pre_ready, it * (TURN * UNIT) + h * UNIT + s + (1, 1, 2, 4)[s])
                pe.matmul(ps[:, EA_BANKS[s]], eaT[:, h % 2, s * P:(s + 1) * P], W1bT,
                          start=True, stop=True).then_inc(ea_done, 1)

            def sums(it, h, span):
                first, end, before = span
                with pe.Fori(first, end) as j:
                    into = ps[:, bass.ds(j, 1)].rearrange("p b n -> p (b n)")
                    pe.wait_ge(lo_ready, it * (TURN * UNIT) + (h + 2) * UNIT)
                    for s in range(UNIT):
                        pe.wait_ge(oh_ready, (j + before) * UNIT + s + 1)
                        pe.matmul(into, oh[:, h % 2, s], rhi[:, h % 2, s], start=False, stop=True, skip_group_check=True)
                        pe.matmul(into, oh[:, h % 2, s], rlo[:, h % 2, s], start=False, stop=True, skip_group_check=True
                                  ).then_inc(oh_free, 1)
                pe.matmul(ps[:, 0, 0:64], zer[:, 0:P], zer[:, 0:64], start=False, stop=True,
                          skip_group_check=True).then_inc(sums_done, 1)

            def unit(it, h):
                attributes(it, h + 1, 0)
                attributes(it, h + 1, 1)
                span = windows(pe, it * TURN + h)
                attributes(it, h + 1, 2)
                sums(it, h, span)
                attributes(it, h + 1, 3)

            def compose(bank, layer, tile):
                for half in range(2):
                    c = 2 * (layer * WT + tile) + half
                    pe.wait_ge(basis_in[c % SLOTS], 16 * (c // SLOTS + 1 + 3 * (c >= SLOTS)))
                    for s2 in range(2):
                        s = 2 * half + s2
                        for g in range(4):
                            mm = pe.matmul(bank[32 * g:32 * g + 32], sel[:, layer, s],
                                           basis[:, c % SLOTS, g, s2], start=(s == 0), stop=(s == 3),
                                           tile_position=(0, 32 * g))
                    if half == 0:
                        mm.then_inc(basis_used, 1)
                return mm

            pe.wait_ge(ct_drained, NT - 1)
            pe.wait_ge(u_drained, NT)
            pe.wait_ge(w1b_in, 16)
            for s in range(UNIT - 1):
                attributes(0, 0, s)
            pe.wait_ge(sel_ready, 1)
            compose(ps[:, EARLY_BANK], 0, 0).then_inc(early_full, 1)
            pe.wait_ge(ct_drained, NT)
            pe.wait_ge(early_drained, 1)
            for n in range(NT):
                pe.matmul(ps[:, n], zer[:, 0:P], zer, start=True, stop=True)
            attributes(0, 0, UNIT - 1)
            with pe.Fori(0, TURNS - 1) as it:
                for h in range(TURN):
                    unit(it, h)
            for h in range(TURN - 1):
                unit(TURNS - 1, h)
            bounds = windows(pe, UNITS - 1)
            name = jobs.list[0][0]
            pe.wait_ge(pre_ready, ET + 4)
            compose(ps[:, jobs.bank(name)], name[1], name[2]).then_inc(bank_full, 1)
            sums(TURNS - 1, TURN - 1, bounds)
            pe.matmul(ps[:, 6, 0:64], zer[:, 0:P], zer[:, 0:64], start=True, stop=True).then_inc(r_acc, 1)

            def products(bank, m, hi, lo, start=True, stop=False):
                terms = [(a, w, k) for a, w in ((xT_hi, hi), (xT_hi, lo), (xT_lo, hi)) for k in range(KT)]
                for i, (a, w, k) in enumerate(terms):
                    mm = pe.matmul(bank, a[:, k, m * P:(m + 1) * P], w[:, k], start=(start and i == 0),
                                   stop=(stop and i == len(terms) - 1))
                return mm

            for n, (name, _) in enumerate(jobs.list):
                kind = name[0]
                bank = ps[:, jobs.bank(name)]
                if n == 0:
                    continue
                if n >= 8:
                    drained_by(pe, jobs.list[n - 8][0])
                if name == ("M", 0, 0, 0):
                    pe.wait_ge(flag_ready, 1)
                    many = pe.value_load(flag[0:1, 0:1], min_val=0, max_val=1)
                if kind == "RT":
                    pe.wait_ge(r_drained, name[1] + 1)
                    for k in range(KT):
                        mm = pe.transpose(bank[:, k * P:(k + 1) * P], R_v[:, name[1], k * P:(k + 1) * P],
                                          ident[:])
                elif kind == "cnt":
                    a, b = ((0, 3), (3, NT))[name[1]]
                    for m in range(a, b):
                        mm = pe.matmul(bank[0:1, (m - a) * P:(m - a + 1) * P], cnt[:, m:m + 1], ident[:],
                                       start=True, stop=True)
                elif kind == "agg":
                    _, o, h = name
                    if (o, h) == (0, 0):
                        for q in range(NT):
                            drained_by(pe, ("RT", q))
                        drained_by(pe, ("cnt", 1))
                        pe.wait_ge(rows_in, 16)
                        pe.wait_ge(w2_in, 16)
                    cols = slice(h * HALF, (h + 1) * HALF)
                    pe.matmul(bank[:, 0:HALF], rows[0:1, o * P:(o + 1) * P], cntrow[0:1, cols],
                              start=True, stop=False)
                    for k in range(KT):
                        mm = pe.matmul(bank[:, 0:HALF], W2T[:, k, o * P:(o + 1) * P], RT[:, k, cols],
                                       start=False, stop=(k == KT - 1))
                elif kind in ("r", "z", "hn", "in"):
                    m = name[1]
                    if kind == "r" and m == 0:
                        pe.wait_ge(gru_in, 32)
                        drained_by(pe, ("agg", KT - 1, 0))
                        drained_by(pe, ("agg", KT - 1, 1))
                    q = {"r": 0, "z": 1, "hn": 2, "in": 2}[kind]
                    cols = slice(q * H, (q + 1) * H)
                    if kind == "hn":
                        add_bias(bank, 0, q, pick=1)
                    else:
                        add_bias(bank, 0, q, 4 if kind in "rz" else 2)
                    parts = [(aggT, WihT)] * (kind != "hn") + [(xT, WhhT)] * (kind != "in")
                    for i, (a, w) in enumerate(parts):
                        for k in range(KT):
                            mm = pe.matmul(bank, a[:, k, m * P:(m + 1) * P], w[:, k, cols], start=False,
                                           stop=(i == len(parts) - 1 and k == KT - 1))
                elif kind == "w":
                    _, layer, tile = name
                    mm = compose(bank, layer, tile)
                elif kind == "xT":
                    _, layer, m = name
                    if layer == 0:
                        pe.wait_ge(x1_ready, m + 1)
                        src = x1
                    else:
                        drained_by(pe, ("out", 0, m))
                        src = h1
                    for k in range(KT):
                        mm = pe.transpose(bank[:, k * P:(k + 1) * P], src[:, m, k * P:(k + 1) * P], ident[:])
                elif kind == "M":
                    _, layer, m, r = name
                    drained_by(pe, ("xT", layer, m))
                    if m == 0:
                        pe.wait_ge(w_hi_in, 16 * REL * KT * (layer + 1))
                        pe.wait_ge(w_lo_in[r], 16 * KT * (layer + 1))
                    mm = products(bank, m, w_hi[:, r], w_lo[:, r], stop=True)
                elif kind == "out":
                    _, layer, m = name
                    if m == 0:
                        pe.wait_ge(ct_rounded, NT)
                        pe.wait_ge(root_ready, layer + 1)
                    add_bias(bank, 1, 1 + layer, 2)
                    products(bank, m, root_hi, root_lo, start=False)

                    def sources(counts, dt):
                        for q in range(NT * REL):
                            n, r = q // REL, q % REL
                            if m == 0:
                                drained_by(pe, ("M", layer, n, r))
                            for half in (Mhi, Mlo):
                                last = q == NT * REL - 1 and half is Mlo
                                mm = pe.matmul(bank, counts[:, n, r * NP + m * P:r * NP + (m + 1) * P],
                                               half[:, n, r].bitcast(dt), start=False, stop=last)
                        mm.then_inc(bank_full, 1)

                    with pe.If(many < 1):
                        sources(CT_r, F32R)
                    with pe.If(many > 0):
                        sources(CT, F32)
                    continue
                mm.then_inc(bank_full, 1)


def kernel(**inputs):
    import concourse.bacc as bacc
    from concourse.bass_utils import run_bass_kernel_spmd

    a = {k: np.asarray(v) for k, v in inputs.items()}
    f32 = np.float32

    def edge_columns(v, fill):
        return np.ascontiguousarray(np.concatenate([v, np.full(ET * P - E, fill, v.dtype)]).reshape(ET, P).T)

    def k_tiles(m):
        return np.ascontiguousarray(m.reshape(-1, P, m.shape[1]).transpose(1, 0, 2))

    x = np.concatenate([a["x"], np.zeros((NP - N, H), f32)])
    ea = np.concatenate([a["edge_attr_128"], np.zeros((ET * P - E, ED), f32)])
    W1 = a["L0_gnn_W1"]
    bias = np.zeros((P, 2, H), f32)
    for part in range(3):
        bias[32 * part:32 * part + 2, 0] = a["L0_gnn_b_ih"][part * H:(part + 1) * H]
        bias[32 * part + 2:32 * part + 4, 0] = a["L0_gnn_b_hh"][part * H:(part + 1) * H]
        bias[32 * part:32 * part + 2, 1] = a[("L0_gnn_b1", "L1_gnn_bias1", "L1_gnn_bias2")[part]]
    odd = np.arange(P)[:, None] % 2
    arrays = {
        "bias": bias,
        "halves": np.concatenate([odd, 1 - 2 * odd], axis=1).astype(f32),
        "picks": np.stack([np.ones((P, P), f32), np.tile((np.arange(P)[:, None] % 4 > 1).astype(f32), (1, P))], axis=1),
        "src": edge_columns(a["src"], NP - 1),
        "dst": edge_columns(a["dst"], NP - 1),
        "dstrow": np.ascontiguousarray(edge_columns(a["dst"], NP - 1).T),
        "tab": np.stack(np.broadcast_arrays(np.arange(NT, dtype=f32)[:, None], np.arange(1, ET + 1, dtype=f32),
                                            np.arange(ET, 0, -1, dtype=f32)))[None],
        "typ": edge_columns(a["edge_type_2"], 0),
        "x": k_tiles(x),
        "xT": k_tiles(x.T),
        "eaT": np.ascontiguousarray(ea.T),
        "W1aT": k_tiles(W1[:, :H].T),
        "W1bT": np.ascontiguousarray(W1[:, H:].T),
        "W2T": k_tiles(a["L0_gnn_W2"].T),
        "WihT": k_tiles(a["L0_gnn_W_ih"].T),
        "WhhT": k_tiles(a["L0_gnn_W_hh"].T),
        "rows": a["L0_gnn_b2"][None],
        "gamma": a["L0_gnn_gamma"][None],
        "beta": a["L0_gnn_beta"][None],
        "mean": a["L0_gnn_run_mean"][None],
        "var": a["L0_gnn_run_var"][None],
        "basis1": a["L1_gnn_basis1"],
        "basis2": a["L1_gnn_basis2"],
        "root1": k_tiles(a["L1_gnn_root1"]),
        "root2": k_tiles(a["L1_gnn_root2"]),
        "att": np.ascontiguousarray(np.repeat(np.stack([a["L1_gnn_att1"], a["L1_gnn_att2"]]).transpose(2, 0, 1),
                                              QTR, axis=0)),
        "gw1": a["L1_gnn_gate_w1"].reshape(1, REL, H),
        "gw2": a["L1_gnn_gate_w2"].reshape(1, REL, H),
        "iota": np.tile(np.arange(RN, dtype=np.float16), (P, 1)),
        "ident": np.eye(P, dtype=f32),
        "maskc": np.tile(np.eye(QTR, dtype=f32), (BASES, 1)),
    }
    nc = bacc.Bacc("TRN2", target_bir_lowering=False, num_devices=1)
    ins = {f"in_{k}": np.ascontiguousarray(v) for k, v in arrays.items()}
    t = {k[3:]: nc.dram_tensor(k, v.shape, mybir.dt.from_np(v.dtype), kind="ExternalInput").ap()
         for k, v in ins.items()}
    t["basis"] = [t["basis1"], t["basis2"]]
    t["gw"] = [t["gw1"], t["gw2"]]
    t["root"] = [t["root1"], t["root2"]]
    t["bn"] = [t["gamma"], t["beta"], t["mean"], t["var"]]
    t["u"] = nc.dram_tensor("u_rows", (NP, H), F32, kind="Internal").ap()
    w = [nc.dram_tensor(f"w_layer{i}", (WT, P, 2, H), F32, kind="Internal").ap() for i in range(2)]
    t["w"] = w
    t["out"] = nc.dram_tensor("out_rows", (NP, H), F32, kind="ExternalOutput").ap()
    gnn_kernel(nc, t)
    r = run_bass_kernel_spmd(nc, [ins], core_ids=[0])
    return r.results[0]["out_rows"][:N]
```
